# Optimizing a Trainium2 kernel written in Bass

```python
import numpy as np
import jax
import jax.numpy as jnp

def _softmax(x, axis=-1):
    return jax.nn.softmax(x, axis=axis)

def _gelu(x):
    return jax.nn.gelu(x, approximate=True)

def _silu(x):
    return jax.nn.silu(x)

def _sigmoid(x):
    return jax.nn.sigmoid(x)

def _layernorm(x, axis=-1, eps=1e-05):
    m = jnp.mean(x, axis=axis, keepdims=True)
    v = jnp.var(x, axis=axis, keepdims=True)
    return (x - m) / jnp.sqrt(v + eps)

def _scatter_add(tgt, idx, src, axis=0):
    return tgt.at[idx].add(src)

def _segment_sum(src, seg, n):
    return jax.ops.segment_sum(src, seg, n)
kernel_name = 'mk_gnn_preln_d1_gnn_r8_83c993'

def setup_inputs(seed: int=0):
    np.random.seed(seed)
    _w = jnp.asarray

    def _rec_inputs():
        import jax
        import jax.numpy as jnp
        _gk = jax.random.key(seed)
        x = -0.0005121 + 1.001 * jax.random.normal(jax.random.fold_in(_gk, 1), (12500, 32), jnp.float32)
        _s = jax.random.randint(jax.random.fold_in(_gk, 2), (200000,), 0, 12500, jnp.int32)
        _d = jax.random.randint(jax.random.fold_in(_gk, 3), (200000,), 0, 12500, jnp.int32)
        _loop = jnp.arange(12500, dtype=jnp.int32)
        src = jnp.concatenate([_s, _d, _loop])
        dst = jnp.concatenate([_d, _s, _loop])
        _o = jnp.argsort(dst, stable=True)
        src = src[_o]
        dst = dst[_o]
        edge_attr_4 = 0.000398945 + 1.00003 * jax.random.normal(jax.random.fold_in(_gk, 11), (412500, 4), jnp.float32)
        return (x, src, dst, edge_attr_4)
    x, src, dst, edge_attr_4 = _rec_inputs()

    def _L0_gnn_setup():
        import jax, jax.numpy as jnp
        import numpy as np
        N_NODES = 12500
        N_EDGES = 200000
        IN_DIM = 32
        HID = 64
        OUT_DIM = 32
        EDGE_DIM = 4
        key = jax.random.key(seed)
        ks = jax.random.split(key, 12)
        x = jax.random.normal(ks[0], (N_NODES, IN_DIM), dtype=jnp.float32)
        edge_index = jax.random.randint(ks[1], (2, N_EDGES), 0, N_NODES, dtype=jnp.int32)
        edge_attr = jax.random.normal(ks[2], (N_EDGES, EDGE_DIM), dtype=jnp.float32)

        def lin(k, fan_in, fan_out):
            kw, kb = jax.random.split(k)
            bound = 1.0 / np.sqrt(fan_in)
            W = jax.random.uniform(kw, (fan_in, fan_out), minval=-bound, maxval=bound, dtype=jnp.float32)
            b = jax.random.uniform(kb, (fan_out,), minval=-bound, maxval=bound, dtype=jnp.float32)
            return (W, b)
        W1, b1 = lin(ks[3], 2 * IN_DIM, HID)
        W2, b2 = lin(ks[4], HID, 2 * HID)
        W3, b3 = lin(ks[5], 2 * HID, HID)
        W4, b4 = lin(ks[6], HID, OUT_DIM)
        return {'x': x, 'edge_index': edge_index, 'edge_attr': edge_attr, 'W1': W1, 'b1': b1, 'W2': W2, 'b2': b2, 'W3': W3, 'b3': b3, 'W4': W4, 'b4': b4}
    _L0_gnn_all = _L0_gnn_setup()
    _L0_gnn_in = {k: v for k, v in _L0_gnn_all.items() if k in ('W1', 'b1', 'W2', 'b2', 'W3', 'b3', 'W4', 'b4')}
    del _L0_gnn_all
    return {'x': x, 'src': src, 'dst': dst, 'edge_attr_4': edge_attr_4, 'L0_gnn_W1': _L0_gnn_in['W1'], 'L0_gnn_b1': _L0_gnn_in['b1'], 'L0_gnn_W2': _L0_gnn_in['W2'], 'L0_gnn_b2': _L0_gnn_in['b2'], 'L0_gnn_W3': _L0_gnn_in['W3'], 'L0_gnn_b3': _L0_gnn_in['b3'], 'L0_gnn_W4': _L0_gnn_in['W4'], 'L0_gnn_b4': _L0_gnn_in['b4']}

def reference(x, src, dst, edge_attr_4, L0_gnn_W1, L0_gnn_b1, L0_gnn_W2, L0_gnn_b2, L0_gnn_W3, L0_gnn_b3, L0_gnn_W4, L0_gnn_b4):
    import jax
    import jax.numpy as jnp

    def _L0_gnn_ref(x, edge_index, edge_attr, W1, b1, W2, b2, W3, b3, W4, b4):
        import jax, jax.numpy as jnp
        import numpy as np
        N_NODES = 12500
        N_EDGES = 200000
        IN_DIM = 32
        HID = 64
        OUT_DIM = 32
        EDGE_DIM = 4
        j_idx = edge_index[0]
        i_idx = edge_index[1]
        x_j = x[j_idx]
        x_i = x[i_idx]
        msg = jnp.concatenate([x_i, x_j - x_i], axis=-1)
        h = jax.nn.relu(msg @ W1 + b1)
        h = jax.nn.relu(h @ W2 + b2)
        h = jax.nn.relu(h @ W3 + b3)
        m = h @ W4 + b4
        s = jax.ops.segment_sum(m, i_idx, num_segments=N_NODES)
        cnt = jax.ops.segment_sum(jnp.ones((m.shape[0],), m.dtype), i_idx, num_segments=N_NODES)
        return s / jnp.maximum(cnt, 1.0)[:, None]
    edge_index = jnp.stack([src, dst])
    h = jnp.maximum(_layernorm(x, axis=-1), 0.0)
    x = x + _L0_gnn_ref(h, edge_index, edge_attr_4, L0_gnn_W1, L0_gnn_b1, L0_gnn_W2, L0_gnn_b2, L0_gnn_W3, L0_gnn_b3, L0_gnn_W4, L0_gnn_b4)
    return x

_drawn_inputs = setup_inputs


def setup_inputs(seed=0):
    import zlib

    import numpy as np

    out = dict(_drawn_inputs(seed))
    spreads = {}
    factors = {'L0_gnn_W1': 4.219,
     'L0_gnn_b1': 8.0,
     'L0_gnn_W2': 3.007,
     'L0_gnn_b2': 5.659,
     'L0_gnn_b3': 2.688}
    for name, (base, spread) in spreads.items():
        noise = np.random.default_rng([zlib.crc32(name.encode()), seed]).standard_normal(out[name].shape)
        drawn = base * np.exp(spread * noise) if base else spread * noise
        out[name] = jnp.asarray(drawn.astype(out[name].dtype))
    for name, factor in factors.items():
        out[name] = (out[name] * factor).astype(out[name].dtype)
    return out
```

```python
import concourse.bass as bass
from concourse import mybir
from concourse.alu_op_type import AluOpType as ALU
from contextlib import ExitStack



def build(nc, x, src, dst, W1, b1, W2, b2, W3, b3, W4, b4, out):
    fp32, bf16, i32 = mybir.dt.float32, mybir.dt.bfloat16, mybir.dt.int32
    ACT = mybir.ActivationFunctionType
    AX = mybir.AxisListType

    P = 128
    N, D = x.shape
    E = src.shape[0]
    H1, H2 = W2.shape
    H3 = W3.shape[1]
    DO = W4.shape[1]
    EPS = 1e-5

    NP, NC = 125, N // 125
    NQ = 4
    CH = 5
    KC = NC // (NQ * CH)
    CW = NQ * CH

    T = 4
    GE = T * P
    GR = 8
    G = -(-E // (GE * GR)) * GR
    QP = G // GR
    RL = GR * GE
    LAST = E - (QP - 1) * RL
    U = 4
    W = 32
    PAD_DST = 1 << 20
    KA = 3 * W

    NT = -(-E // P)
    HX = H3 + 1

    def dram(name, shape, dt):
        return nc.dram_tensor(name, shape, dt, kind="Internal").ap()

    A_tab = dram("A_tab", (N * 3, H1), bf16)
    B_tab = dram("B_tab", (N, H1), fp32)
    base_tab = dram("base_tab", (G,), i32)
    dst_pad = dram("dst_pad", (QP * RL,), i32)
    src_pad = dram("src_pad", (QP * RL,), i32)
    sum_tab = dram("sum_tab", (N, HX), fp32)

    ctx = ExitStack()
    with ctx:
        def sb(name, shape, dt=fp32):
            return ctx.enter_context(nc.sbuf_tensor(name, shape, dt))

        def sem(name):
            return ctx.enter_context(nc.semaphore(name))

        bank = [ctx.enter_context(nc.psum_tensor(f"bank{i}", [P, 512], fp32)) for i in range(8)]

        x_sb = sb("x_sb", [NP, NC * D])
        big = sb("big", [P, N])
        cen = big[0:NP, 0:NC * D]
        src_raw = big[0:QP, NC * D:NC * D + RL]
        dst_raw = big[0:QP, NC * D + RL:NC * D + 2 * RL]
        acc = big[0:HX, :]
        src_T = sb("src_T", [P, G, T], i32)
        rel_T = sb("rel_T", [P, G, T])
        base_bc = sb("base_bc", [P, G], i32)
        base_row = sb("base_row", [1, G], i32)
        ident = sb("ident", [P, P])
        iota_w = sb("iota_w", [P, T, W, 3])
        zeros = sb("zeros", [HX, 500])
        w2 = sb("w2", [H1, H2])
        w3 = sb("w3", [H2, H3])
        w4 = sb("w4", [HX, DO + 1])
        b2c = sb("b2c", [H2, 1])
        b3_row = sb("b3_row", [1, H3])
        b3_p = sb("b3_p", [1, 3, H3], bf16)
        b3_r = sb("b3_r", [1, H3])
        b3_rep = sb("b3_rep", [1, 3, T, H3], bf16)
        b3_k = sb("b3_k", [3, T * H3], bf16)
        ones_b = sb("ones_b", [3, P], bf16)
        eps_c = sb("eps_c", [P, 1])
        flag_i = sb("flag_i", [1, 1], i32)

        x_in, src_in, dst_in, w_in = sem("x_in"), sem("src_in"), sem("dst_in"), sem("w_in")
        pool_const, pads_set = sem("pool_const"), sem("pads_set")
        dch = sem("dch")
        cen_ready, sq_ready, ssq_ready, sd_ready = sem("cen_ready"), sem("sq_ready"), sem("ssq_ready"), sem("sd_ready")
        h_ready, bd_ready = sem("h_ready"), sem("bd_ready")
        src_fp, dst_fp, idx_tr, src_cp, dst_cp = sem("src_fp"), sem("dst_fp"), sem("idx_tr"), sem("src_cp"), sem("dst_cp")
        hT_tr, hT_cp, tab_mm, tabB_cp, tabA_cp = sem("hT_tr"), sem("hT_cp"), sem("tab_mm"), sem("tabB_cp"), sem("tabA_cp")
        B_out = [sem("B_out0"), sem("B_out1")]
        A_hi, A_r1, A_mid, A_lo = sem("A_hi"), sem("A_r1"), sem("A_mid"), sem("A_lo")
        A_out = [sem("A_out0"), sem("A_out1")]
        base_ready, base_out, base_in, baseb_in = sem("base_ready"), sem("base_out"), sem("base_in"), sem("baseb_in")
        bad_ready, bad_mm, flag_ready = sem("bad_ready"), sem("bad_mm"), sem("flag_ready")
        b3_ready, b3_in = sem("b3_ready"), sem("b3_in")
        acc_zero, zero_set, pads_out = sem("acc_zero"), sem("zero_set"), sem("pads_out")

        prep = ExitStack()
        with prep:
            def psb(name, shape, dt=fp32):
                return prep.enter_context(nc.sbuf_tensor(name, shape, dt))

            sq = psb("sq", [NP, CW * D])
            st = psb("st", [NP, 4, CW])
            B_sb = psb("B_sb", [NP, 2, CW, H1])
            A_f = psb("A_f", [NP, NC, H1])
            A_r = psb("A_r", [NP, 2, CW, H1])
            A_p = psb("A_p", [NP, 2, CW, 3, H1], bf16)
            hT = psb("hT", [P, CH, NP])
            w1a = psb("w1a", [P, H1])
            w1b = psb("w1b", [P, H1])
            w1_bd = psb("w1_bd", [P, 2, NQ, H1])
            b1_bc = psb("b1_bc", [NP, H1])
            mn = psb("mn", [QP, GR])
            base_f = psb("base_f", [QP, GR])
            base_i = psb("base_i", [QP, GR], i32)
            mx = psb("mx", [QP, GR + 1])
            span = psb("span", [QP, GR + 1])
            bad = psb("bad", [P, 1])
            ones_f = psb("ones_f", [P, 1])
            src_i = src_raw.bitcast(i32)
            dst_i = dst_raw.bitcast(i32)

            block = prep.enter_context(nc.Block())
            hT_ps, A_ps, B_ps = bank[2:4], bank[4:6], bank[6:8]

            @block.gpsimd
            def _(pool):
                pad0 = (QP - 1) // 32 * 32
                nc.gpsimd.memset(src_i[pad0:QP, LAST:RL], 0).then_inc(pads_set, 1)
                nc.gpsimd.memset(dst_i[pad0:QP, LAST:RL], PAD_DST).then_inc(pads_set, 1)
                pool.wait_ge(pads_set, 2)
                nc.gpsimd.memset(zeros[:], 0.0).then_inc(zero_set, 1)
                nc.gpsimd.memset(ident[:], 0.0).then_inc(pool_const, 1)
                pool.wait_ge(pool_const, 1)
                nc.gpsimd.affine_select(out=ident[:], in_=ident[:], compare_op=ALU.not_equal, fill=1.0, base=0,
                                        pattern=[[-1, P]], channel_multiplier=1).then_inc(pool_const, 1)
                nc.gpsimd.iota(iota_w[:], pattern=[[0, T], [1, W], [0, 3]], base=0, channel_multiplier=0,
                               allow_small_or_imprecise_dtypes=True).then_inc(pool_const, 1)
                nc.gpsimd.memset(ones_b[:], 1.0).then_inc(pool_const, 1)
                nc.gpsimd.memset(ones_f[:], 1.0).then_inc(pool_const, 1)

            @block.sync
            def _(sp):
                sp.dma_start(x_sb[:], x.rearrange("(p c) d -> p (c d)", p=NP)).then_inc(x_in, 16)
                sp.wait_ge(pads_set, 2)
                for raw, arr, s in ((src_i, src, src_in), (dst_i, dst, dst_in)):
                    sp.dma_start(raw[0:QP - 1, :], arr[0:(QP - 1) * RL].rearrange("(q e) -> q e", e=RL)).then_inc(s, 16)
                    sp.dma_start(raw[QP - 1:QP, 0:LAST], arr[(QP - 1) * RL:E].rearrange("(q e) -> q e", q=1)).then_inc(s, 16)
                sp.wait_ge(base_ready, 1)
                sp.dma_start(base_tab.rearrange("(q r) -> q r", r=GR), base_i[:]).then_inc(base_out, 16)
                sp.wait_ge(base_out, 16)
                sp.dma_start(base_bc[:], base_tab.partition_broadcast(P)).then_inc(baseb_in, 16)
                sp.dma_start(base_row[:], base_tab.rearrange("(o g) -> o g", o=1)).then_inc(base_in, 16)
                sp.wait_ge(b3_ready, 1)
                for k in range(3):
                    sp.dma_start(b3_k[k:k + 1, :], b3_rep[:, k, :, :].rearrange("o t d -> o (t d)")).then_inc(b3_in, 16)
                Bv = B_tab.rearrange("(p c) d -> p c d", p=NP)
                for k in range(KC):
                    sp.wait_ge(tabB_cp, CH * (k + 1))
                    sp.dma_start(Bv[:, k * CW:(k + 1) * CW, :], B_sb[:, k % 2, :, :]).then_inc(B_out[k % 2], 16)
                Av = A_tab.rearrange("(p c k) d -> p c k d", p=NP, k=3)
                for k in range(KC):
                    sp.wait_ge(A_lo, k + 1)
                    sp.dma_start(Av[:, k * CW:(k + 1) * CW, :, :], A_p[:, k % 2, :, :, :]).then_inc(A_out[k % 2], 16)
                sp.wait_ge(hT_tr, KC * CH)
                sp.wait_ge(idx_tr, 2 * GR)
                sp.wait_ge(pads_out, 32)
                sp.wait_ge(zero_set, 1)
                for c in range(0, N, 2500):
                    sp.dma_start(acc[:, c:c + 2500].rearrange("p (a b) -> p a b", b=500),
                                 zeros[:].unsqueeze(1).to_broadcast([HX, 5, 500])).then_inc(acc_zero, 16)
                sp.wait_ge(acc_zero, 16 * 5)
                sp.wait_ge(B_out[0], 16 * 3)
                sp.wait_ge(B_out[1], 16 * 2)
                sp.wait_ge(A_out[0], 16 * 3)
                sp.wait_ge(A_out[1], 16 * 2)
                sp.wait_ge(base_in, 16)
                sp.wait_ge(b3_in, 48)

            @block.scalar
            def _(act):
                for c in range(NQ):
                    act.dma_start(w1a[c * D:(c + 1) * D, :], W1[0:D, :]).then_inc(w_in, 16)
                    act.dma_start(w1b[c * D:(c + 1) * D, :], W1[D:2 * D, :]).then_inc(w_in, 16)
                act.dma_start(b1_bc[:], b1.partition_broadcast(NP)).then_inc(w_in, 16)
                act.dma_start(w2[:], W2).then_inc(w_in, 16)
                act.dma_start(w3[:], W3).then_inc(w_in, 16)
                act.dma_start(w4[0:H3, 0:DO], W4).then_inc(w_in, 16)
                act.dma_start(w4[H3:HX, 0:DO], b4.rearrange("(o d) -> o d", o=1)).then_inc(w_in, 16)
                act.dma_start(b2c[:], b2.rearrange("(d o) -> d o", o=1)).then_inc(w_in, 16)
                act.dma_start(b3_row[:], b3.rearrange("(o d) -> o d", o=1)).then_inc(w_in, 16)
                act.wait_ge(src_in, 32)
                act.dma_start(src_pad.rearrange("(q e) -> q e", e=RL), src_i).then_inc(pads_out, 16)
                act.wait_ge(dst_in, 32)
                act.dma_start(dst_pad.rearrange("(q e) -> q e", e=RL), dst_i).then_inc(pads_out, 16)

                def square(k):
                    act.wait_ge(cen_ready, k + 1)
                    nc.scalar.activation(sq[:], cen[:, bass.ds(k * CW * D, CW * D)], ACT.Square).then_inc(sq_ready, 1)

                def deviation(k):
                    act.wait_ge(ssq_ready, k + 1)
                    nc.scalar.activation(st[:, 3, :], st[:, 2, :], ACT.Sqrt, bias=eps_c[0:NP, :], scale=1.0 / D).then_inc(sd_ready, 1)

                act.wait_ge(bd_ready, 1)
                square(0)
                deviation(0)
                act.wait_ge(pads_out, 32)
                nc.scalar.activation(src_raw, src_i, ACT.Copy).then_inc(src_fp, 1)
                square(1)
                deviation(1)
                for r in range(GR):
                    act.wait_ge(idx_tr, r + 1)
                    nc.scalar.activation(src_T[:, :, :].rearrange("p (q r) j -> p r j q", r=GR)[:, r, :, :],
                                         bank[r % 2][:, 0:T * QP].rearrange("p (j q) -> p j q", j=T), ACT.Copy).then_inc(src_cp, 1)
                for k in range(KC):
                    for u in range(CH):
                        n = k * CH + u
                        act.wait_ge(hT_tr, n + 1)
                        if n >= CH:
                            act.wait_ge(tab_mm, n - CH + 1)
                        nc.scalar.activation(hT[:, u, :], hT_ps[n % 2][:, 0:NP], ACT.Copy).then_inc(hT_cp, 1)
                        act.wait_ge(tab_mm, n + 1)
                        if u == 0 and k >= 2:
                            act.wait_ge(B_out[k % 2], 16 * (k // 2))
                        nc.scalar.activation(B_sb[:, k % 2, NQ * u:NQ * (u + 1), :],
                                             B_ps[n % 2][0:NP, 0:NQ * H1].rearrange("p (c w) -> p c w", c=NQ),
                                             ACT.Copy).then_inc(tabB_cp, 1)
                    if k + 2 < KC:
                        square(k + 2)
                        deviation(k + 2)
                for k in range(KC):
                    act.wait_ge(tabA_cp, CH * (k + 1))
                    if k >= 2:
                        act.wait_ge(A_out[k % 2], 16 * (k // 2))
                    nc.scalar.activation(A_p[:, k % 2, :, 0, :], A_f[:, k * CW:(k + 1) * CW, :], ACT.Copy).then_inc(A_hi, 1)
                    act.wait_ge(A_r1, k + 1)
                    nc.scalar.activation(A_p[:, k % 2, :, 1, :], A_r[:, k % 2, :, :], ACT.Copy).then_inc(A_mid, 1)

            @block.tensor
            def _(pe):
                pe.wait_ge(pool_const, 5)
                def index_rows(n, raw):
                    r = n % GR
                    for j in range(T):
                        last = nc.tensor.transpose(bank[n % 2][:, j * QP:(j + 1) * QP],
                                                   raw[:, r * GE + j * P:r * GE + (j + 1) * P], ident[0:QP, 0:QP])
                    last.then_inc(idx_tr, 1)

                pe.wait_ge(src_fp, 1)
                for r in range(GR):
                    if r >= 2:
                        pe.wait_ge(src_cp, r - 1)
                    index_rows(r, src_raw)
                pe.wait_ge(bd_ready, 2)
                for k in range(KC):
                    pe.wait_ge(h_ready, k + 1)
                    for u in range(CH):
                        n = k * CH + u
                        if n >= 2:
                            pe.wait_ge(hT_cp, n - 1)
                        nc.tensor.transpose(hT_ps[n % 2][:, 0:NP], cen[:, n * NQ * D:(n + 1) * NQ * D],
                                            ident[0:NP, 0:NP]).then_inc(hT_tr, 1)
                        pe.wait_ge(hT_cp, n + 1)
                        for i, (ps, cp) in enumerate(((A_ps, tabA_cp), (B_ps, tabB_cp))):
                            if n >= 2:
                                pe.wait_ge(cp, n - 1)
                            last = nc.tensor.matmul(ps[n % 2][0:NP, 0:NQ * H1], hT[:, u, :],
                                                    w1_bd[:, i, :, :].rearrange("p c w -> p (c w)"), start=True, stop=True)
                        last.then_inc(tab_mm, 1)
                pe.wait_ge(dst_fp, 1)
                for r in range(GR):
                    if r < 2:
                        pe.wait_ge(src_cp, GR - 1 + r)
                    else:
                        pe.wait_ge(dst_cp, r - 1)
                    index_rows(GR + r, dst_raw)
                pe.wait_ge(bad_ready, 1)
                pe.wait_ge(tabB_cp, KC * CH)
                pe.wait_ge(tabA_cp, KC * CH)
                nc.tensor.matmul(bank[7][0:1, 0:1], bad[:], ones_f[:], start=True, stop=True).then_inc(bad_mm, 1)

            @block.vector
            def _(dve):
                chain = [0]

                def link(ins):
                    chain[0] += 1
                    ins.then_inc(dch, 1)
                    dve.wait_ge(dch, chain[0])

                nc.vector.memset(eps_c[:], EPS).then_inc(bd_ready, 1)
                link(nc.vector.memset(w4[0:H3, DO:DO + 1], 0.0))
                link(nc.vector.memset(w4[H3:HX, DO:DO + 1], 1.0))
                link(nc.vector.memset(bad[:], 0.0))
                link(nc.vector.memset(w1_bd[:], 0.0))

                def layernorm(k):
                    xs = x_sb[:, k * CW * D:(k + 1) * CW * D].rearrange("p (c d) -> p c d", d=D)
                    cs = cen[:, k * CW * D:(k + 1) * CW * D].rearrange("p (c d) -> p c d", d=D)
                    link(nc.vector.tensor_reduce(st[:, 0, :], xs, AX.X, ALU.add))
                    link(nc.vector.tensor_scalar(st[:, 1, :], st[:, 0, :], -1.0 / D, None, ALU.mult))
                    nc.vector.tensor_tensor(cs, xs, st[:, 1, :].unsqueeze(2).to_broadcast([NP, CW, D]), ALU.add).then_inc(cen_ready, 1)
                    dve.wait_ge(sq_ready, k + 1)
                    nc.vector.tensor_reduce(st[:, 2, :], sq[:].rearrange("p (c d) -> p c d", d=D), AX.X, ALU.add).then_inc(ssq_ready, 1)
                    dve.wait_ge(sd_ready, k + 1)
                    link(nc.vector.reciprocal(st[:, 3, :], st[:, 3, :]))
                    nc.vector.scalar_tensor_tensor(out=cs, in0=cs, scalar=0.0, in1=st[:, 3, :].unsqueeze(2).to_broadcast([NP, CW, D]),
                                                   op0=ALU.max, op1=ALU.mult).then_inc(h_ready, 1)

                dve.wait_ge(x_in, 16)
                layernorm(0)
                dve.wait_ge(w_in, 16 * 15)
                for c in range(NQ):
                    rows = slice(c * D, (c + 1) * D)
                    nc.vector.tensor_tensor(w1_bd[rows, 0, c, :], w1a[rows, :], w1b[rows, :], ALU.subtract)
                    last = nc.vector.tensor_copy(w1_bd[rows, 1, c, :], w1b[rows, :])
                last.then_inc(bd_ready, 1)
                link(nc.vector.tensor_copy(b3_p[:, 0, :], b3_row[:]))
                link(nc.vector.tensor_tensor(b3_r[:], b3_row[:], b3_p[:, 0, :], ALU.subtract))
                link(nc.vector.tensor_copy(b3_p[:, 1, :], b3_r[:]))
                link(nc.vector.tensor_tensor(b3_p[:, 2, :], b3_r[:], b3_p[:, 1, :], ALU.subtract))
                nc.vector.tensor_copy(b3_rep[:], b3_p[:].unsqueeze(2).to_broadcast([1, 3, T, H3])).then_inc(b3_ready, 1)
                layernorm(1)
                dve.wait_ge(dst_in, 32)
                dv = dst_i.rearrange("q (r e) -> q r e", r=GR)
                link(nc.vector.tensor_reduce(mn[:], dv, AX.X, ALU.min))
                link(nc.vector.tensor_scalar(base_f[:], mn[:], float(N - W), None, ALU.min))
                nc.vector.tensor_copy(base_i[:], base_f[:]).then_inc(base_ready, 1)

                def take_A(k):
                    for u in range(CH):
                        n = k * CH + u
                        dve.wait_ge(tab_mm, n + 1)
                        nc.vector.tensor_tensor(A_f[:, NQ * n:NQ * (n + 1), :],
                                                A_ps[n % 2][0:NP, 0:NQ * H1].rearrange("p (c w) -> p c w", c=NQ),
                                                b1_bc[:].unsqueeze(1).to_broadcast([NP, NQ, H1]), ALU.add).then_inc(tabA_cp, 1)

                for k in range(KC):
                    take_A(k)
                    if k + 2 < KC:
                        layernorm(k + 2)
                full, part = LAST // GE, LAST % GE
                link(nc.vector.memset(mx[:], 0.0))
                link(nc.vector.tensor_reduce(mx[:, 0:full], dv[:, 0:full, :], AX.X, ALU.max))
                link(nc.vector.tensor_reduce(mx[0:QP - 1, full:GR], dv[0:QP - 1, full:GR, :], AX.X, ALU.max))
                if part:
                    link(nc.vector.tensor_reduce(mx[:, GR:GR + 1], dv[:, full, 0:part].unsqueeze(1), AX.X, ALU.max))
                link(nc.vector.tensor_tensor(span[:, 0:GR], mx[:, 0:GR], base_f[:], ALU.subtract))
                link(nc.vector.tensor_tensor(span[:, GR:GR + 1], mx[:, GR:GR + 1], base_f[:, min(full, GR - 1):min(full, GR - 1) + 1], ALU.subtract))
                link(nc.vector.tensor_reduce(mn[:, 0:1], span[:], AX.X, ALU.max))
                nc.vector.tensor_scalar(bad[0:QP, :], mn[:, 0:1], float(W), None, ALU.is_ge).then_inc(bad_ready, 1)
                dve.wait_ge(pads_out, 32)
                nc.vector.tensor_copy(dst_raw, dst_i).then_inc(dst_fp, 1)
                for k in range(KC):
                    dve.wait_ge(A_hi, k + 1)
                    nc.vector.tensor_tensor(A_r[:, k % 2, :, :], A_f[:, k * CW:(k + 1) * CW, :], A_p[:, k % 2, :, 0, :],
                                            ALU.subtract).then_inc(A_r1, 1)
                    dve.wait_ge(A_mid, k + 1)
                    nc.vector.tensor_tensor(A_p[:, k % 2, :, 2, :], A_r[:, k % 2, :, :], A_p[:, k % 2, :, 1, :],
                                            ALU.subtract).then_inc(A_lo, 1)
                dve.wait_ge(baseb_in, 16)
                for r in range(GR):
                    dve.wait_ge(idx_tr, GR + r + 1)
                    nc.vector.tensor_tensor(rel_T[:, :, :].rearrange("p (q r) j -> p r j q", r=GR)[:, r, :, :],
                                            bank[r % 2][:, 0:T * QP].rearrange("p (j q) -> p j q", j=T),
                                            base_bc[:].rearrange("p (q r) -> p r q", r=GR)[:, r, :].unsqueeze(1).to_broadcast([P, T, QP]),
                                            ALU.subtract).then_inc(dst_cp, 1)
                dve.wait_ge(bad_mm, 1)
                nc.vector.tensor_copy(flag_i[:], bank[7][0:1, 0:1]).then_inc(flag_ready, 1)
                dve.wait_ge(flag_ready, 1)

        flag = nc.values_load(flag_i[0:1, 0:1], min_val=0, max_val=P)

        def unless_zero(eng, s, count):
            if not isinstance(count, int) or count > 0:
                eng.wait_ge(s, count)

        with nc.If(flag == 0):
            fast = ExitStack()
            with fast:
                def fsb(name, shape, dt=fp32):
                    return fast.enter_context(nc.sbuf_tensor(name, shape, dt))

                def fsem(name):
                    return fast.enter_context(nc.semaphore(name))

                idx = fsb("idx", [P, U, T], i32)
                B_g = fsb("B_g", [P, U, T, H1])
                A_w = fsb("A_w", [KA, U, H1], bf16)
                O = fsb("O", [P, U, T, W, 3])
                OT = fsb("OT", [KA, 2, GE], bf16)
                h1 = fsb("h1", [H1, 2, GE])
                h2 = fsb("h2", [H2, 2, GE])
                h3 = fsb("h3", [P, 2, T, HX])
                z1, z2, z3 = bank[0:2], bank[2:4], bank[4:6]
                ot_ps = bank[6]
                seg = bank[7]

                idx_ready, turn = fsem("idx_ready"), fsem("turn")
                b_in = [fsem(f"b_in{u}") for u in range(U)]
                a_in = [fsem(f"a_in{u}") for u in range(U)]
                ones_set = fsem("ones_set")
                o_ready, ot_ready, otc_ready = fsem("o_ready"), fsem("ot_ready"), fsem("otc_ready")
                z1_ready, z2_ready, z3_ready, seg_ready = fsem("z1_ready"), fsem("z2_ready"), fsem("z3_ready"), fsem("seg_ready")
                h1_ready, h2_ready, h3_ready, acc_done = fsem("h1_ready"), fsem("h2_ready"), fsem("h3_ready"), fsem("acc_done")

                def live(g):
                    return not isinstance(g, int) or 0 <= g < G

                def groups(eng, step, first=0, after=0):
                    for g in range(first, U):
                        step(g, g % U)
                    with eng.Fori(1, G // U - 1) as i:
                        for u in range(U):
                            step(i * U + u, u)
                    for g in range(G - U, G + after):
                        step(g, g % U)

                fblock = fast.enter_context(nc.Block())

                @fblock.sync
                def _(sp):
                    def step(g, u):
                        unless_zero(sp, z1_ready, g - U + 1)
                        first = sp.value_load(base_row[0:1, bass.ds(g, 1)], min_val=0, max_val=N - W)
                        sp.dma_start(A_w[:, u, :], A_tab[bass.ds(first * 3, KA), :]).then_inc(a_in[u], 16)
                    groups(sp, step)

                @fblock.gpsimd
                def _(pool):
                    def step(g, u):
                        pool.wait_ge(idx_ready, g + 1)
                        pool.sem_inc(turn, 1)
                        for j in range(T):
                            nc.gpsimd.indirect_dma_start(
                                out=B_g[:, u, j, :], out_offset=None, in_=B_tab[:, :],
                                in_offset=bass.IndirectOffsetOnAxis(ap=idx[:, u, j:j + 1], axis=0)).then_inc(b_in[u], 16)
                    groups(pool, step)

                @fblock.tensor
                def _(pe):
                    def step(g, u):
                        if live(g - 3):
                            s, b = (u - 3) % U, (u - 3) % 2
                            pe.wait_ge(h3_ready, g - 2)
                            unless_zero(pe, acc_done, g - 3)
                            for j in range(T):
                                last = nc.tensor.matmul(seg[0:HX, 0:W], h3[:, b, j, :], O[:, s, j, :, 0],
                                                        start=(j == 0), stop=(j == T - 1))
                            last.then_inc(seg_ready, 1)
                        if live(g - 2):
                            b = (u - 2) % 2
                            pe.wait_ge(h2_ready, g - 1)
                            unless_zero(pe, h3_ready, g - 3)
                            nc.tensor.matmul(z3[b][:, 0:T * H3], ones_b[:], b3_k[:], start=True, stop=False)
                            for j in range(T):
                                last = nc.tensor.matmul(z3[b][:, j * H3:(j + 1) * H3], h2[:, b, j * P:(j + 1) * P], w3[:],
                                                        start=False, stop=(j == T - 1))
                            last.then_inc(z3_ready, 1)
                        if live(g - 1):
                            b = (u - 1) % 2
                            pe.wait_ge(h1_ready, g)
                            unless_zero(pe, h2_ready, g - 2)
                            nc.tensor.matmul(z2[b][:, :], w2[:], h1[:, b, :], start=True, stop=True).then_inc(z2_ready, 1)
                        if live(g):
                            b = u % 2
                            pe.wait_ge(otc_ready, g + 1)
                            pe.wait_ge(a_in[u], (g - u) * 4 + 16)
                            unless_zero(pe, h1_ready, g - 1)
                            nc.tensor.matmul(z1[b][0:H1, :], A_w[:, u, :], OT[:, b, :], start=True, stop=False)
                            pe.wait_ge(b_in[u], (g - u) * 16 + 64)
                            for j in range(T):
                                last = nc.tensor.matmul(z1[b][0:H1, j * P:(j + 1) * P], B_g[:, u, j, :], ident[:],
                                                        start=False, stop=(j == T - 1))
                            last.then_inc(z1_ready, 1)
                        if live(g + 1):
                            s = (u + 1) % U
                            pe.wait_ge(o_ready, g + 2)
                            unless_zero(pe, otc_ready, g + 1)
                            for j in range(T):
                                last = nc.tensor.transpose(ot_ps[0:KA, j * P:(j + 1) * P],
                                                           O[:, s, j, :, :].rearrange("p w k -> p (w k)"), ident[:])
                            last.then_inc(ot_ready, 1)
                    groups(pe, step, first=-1, after=3)

                @fblock.scalar
                def _(act):
                    def ids(g, u):
                        nc.scalar.activation(idx[:, u, :], src_T[:, bass.ds(g, 1), :].rearrange("p g j -> p (g j)"),
                                             ACT.Copy).then_inc(idx_ready, 1)

                    for g in range(U):
                        ids(g, g)

                    def step(g, u):
                        if live(g - 2):
                            b = (u - 2) % 2
                            act.wait_ge(z3_ready, g - 1)
                            if isinstance(g, int) and g == 2:
                                act.wait_ge(ones_set, 1)
                            unless_zero(act, seg_ready, g - 3)
                            nc.scalar.activation(h3[:, b, :, 0:H3], z3[b][:, 0:T * H3].rearrange("p (j d) -> p j d", j=T),
                                                 ACT.Relu).then_inc(h3_ready, 1)
                        if live(g - 1):
                            b = (u - 1) % 2
                            act.wait_ge(z2_ready, g)
                            unless_zero(act, z3_ready, g - 2)
                            nc.scalar.activation(h2[:, b, :], z2[b][:, :], ACT.Relu, bias=b2c[:]).then_inc(h2_ready, 1)
                        if live(g):
                            b = u % 2
                            act.wait_ge(z1_ready, g + 1)
                            unless_zero(act, z2_ready, g - 1)
                            nc.scalar.activation(h1[:, b, :], z1[b][0:H1, :], ACT.Relu).then_inc(h1_ready, 1)
                            if live(g + U):
                                ids(g + U, u)
                    groups(act, step, after=2)

                @fblock.vector
                def _(dve):
                    nc.vector.memset(h3[:], 1.0).then_inc(ones_set, 1)

                    def step(g, u):
                        if live(g - 3):
                            dve.wait_ge(seg_ready, g - 2)
                            unless_zero(dve, acc_done, g - 3)
                            first = dve.value_load(base_row[0:1, bass.ds(g - 3, 1)], min_val=0, max_val=N - W)
                            nc.vector.tensor_tensor(acc[:, bass.ds(first, W)], seg[0:HX, 0:W], acc[:, bass.ds(first, W)],
                                                    ALU.add).then_inc(acc_done, 1)
                        if live(g + 1):
                            s, b = (u + 1) % U, (u + 1) % 2
                            nc.vector.tensor_tensor(O[:, s, :, :, :].rearrange("p j w k -> p j (w k)"),
                                                    rel_T[:, bass.ds(g + 1, 1), :].rearrange("p g j -> p (g j)").unsqueeze(2).to_broadcast([P, T, KA]),
                                                    iota_w[:].rearrange("p j w k -> p j (w k)"), ALU.is_equal).then_inc(o_ready, 1)
                            dve.wait_ge(ot_ready, g + 2)
                            unless_zero(dve, z1_ready, g)
                            nc.vector.tensor_copy(OT[:, b, :], ot_ps[0:KA, :]).then_inc(otc_ready, 1)
                    groups(dve, step, first=-1, after=3)
                    dve.wait_ge(acc_done, G)

        with nc.Else():
            gen = ExitStack()
            with gen:
                def gsb(name, shape, dt=fp32):
                    return gen.enter_context(nc.sbuf_tensor(name, shape, dt))

                def gsem(name):
                    return gen.enter_context(nc.semaphore(name))

                s_col = gsb("s_col", [P, 1], i32)
                d_col = gsb("d_col", [P, 1], i32)
                d_row = gsb("d_row", [P, P], i32)
                d_clip = gsb("d_clip", [P, 1], i32)
                d_f = gsb("d_f", [P, 1])
                S = gsb("S", [P, P])
                S_low = gsb("S_low", [P, P])
                low = gsb("low", [P, P])
                dup = gsb("dup", [P, 1])
                d_once = gsb("d_once", [P, 1], i32)
                B_r = gsb("B_r", [P, H1])
                A_r = gsb("A_r2", [P, 3, H1], bf16)
                z_e = gsb("z_e", [P, H1])
                g1 = gsb("g1", [H1, P])
                g2 = gsb("g2", [H2, P])
                g3 = gsb("g3", [P, HX])
                old = gsb("old", [P, HX])
                new = gsb("new", [P, HX])
                s_all = gsb("s_all", [NP, NC, HX])
                s_one = gsb("s_one", [NP, HX])

                g_turn = gsem("g_turn")
                low_set, tab_zero, ids_in, clip_ready, rows_in, g_chain = (
                    gsem("low_set"), gsem("tab_zero"), gsem("ids_in"), gsem("clip_ready"), gsem("rows_in"), gsem("g_chain"))
                z_ready, t1, r1, t2, r2, t3, r3, t4 = [gsem(n) for n in ("z_ready", "t1", "r1", "t2", "r2", "t3", "r3", "t4")]
                new_ready, stored, all_in, one_ready, one_tr, one_done = [
                    gsem(n) for n in ("new_ready", "stored", "all_in", "one_ready", "one_tr", "one_done")]
                A_rows = A_tab.rearrange("(n k) d -> n (k d)", k=3)

                gblock = gen.enter_context(nc.Block())

                @gblock.sync
                def _(sp):
                    sp.dma_start(sum_tab.rearrange("n k -> (n k)").rearrange("(p a b) -> p a b", p=HX, b=500),
                                 zeros[:].unsqueeze(1).to_broadcast([HX, N // 500, 500])).then_inc(tab_zero, 16)
                    with sp.Fori(0, NT) as t:
                        sp.wait_ge(stored, t * 16)
                        sp.dma_start(s_col[:], src_pad[bass.ds(t * P, P)].rearrange("(p o) -> p o", o=1)).then_inc(ids_in, 16)
                        sp.dma_start(d_col[:], dst_pad[bass.ds(t * P, P)].rearrange("(p o) -> p o", o=1)).then_inc(ids_in, 16)
                        sp.dma_start(d_row[:], dst_pad[bass.ds(t * P, P)].partition_broadcast(P)).then_inc(ids_in, 16)
                    sp.wait_ge(stored, NT * 16)
                    sp.dma_start(s_all[:], sum_tab.rearrange("(p c) k -> p c k", p=NP)).then_inc(all_in, 16)

                @gblock.gpsimd
                def _(pool):
                    nc.gpsimd.memset(low[:], 1.0).then_inc(low_set, 1)
                    pool.wait_ge(low_set, 1)
                    nc.gpsimd.affine_select(out=low[:], in_=low[:], compare_op=ALU.is_gt, fill=0.0, base=0,
                                            pattern=[[-1, P]], channel_multiplier=1).then_inc(low_set, 1)
                    nc.gpsimd.memset(g3[:], 1.0).then_inc(low_set, 1)
                    with pool.Fori(0, NT) as t:
                        pool.wait_ge(clip_ready, t + 1)
                        pool.wait_ge(tab_zero, 16)
                        pool.sem_inc(g_turn, 1)
                        for o, tab, i in ((B_r[:, :], B_tab[:, :], s_col), (A_r[:].rearrange("p k d -> p (k d)"), A_rows[:, :], d_clip),
                                          (old[:, :], sum_tab[:, :], d_clip)):
                            nc.gpsimd.indirect_dma_start(out=o, out_offset=None, in_=tab,
                                                         in_offset=bass.IndirectOffsetOnAxis(ap=i[:, 0:1], axis=0)).then_inc(rows_in, 16)
                        pool.wait_ge(new_ready, t + 1)
                        pool.sem_inc(g_turn, 1)
                        nc.gpsimd.indirect_dma_start(out=sum_tab[:, :], out_offset=bass.IndirectOffsetOnAxis(ap=d_once[:, 0:1], axis=0),
                                                     in_=new[:, :], in_offset=None, bounds_check=N - 1,
                                                     oob_is_err=False).then_inc(stored, 16)
                    pool.wait_ge(stored, NT * 16)

                @gblock.tensor
                def _(pe):
                    with pe.Fori(0, NT) as t:
                        pe.wait_ge(z_ready, t + 1)
                        pe.sem_inc(g_turn, 1)
                        nc.tensor.transpose(bank[0][0:H1, 0:P], z_e[:], ident[:]).then_inc(t1, 1)
                        pe.wait_ge(r1, t + 1)
                        nc.tensor.matmul(bank[1][:, 0:P], w2[:], g1[:], start=True, stop=True).then_inc(t2, 1)
                        pe.wait_ge(r2, t + 1)
                        nc.tensor.matmul(bank[2][:, 0:H3], ones_b[:], b3_k[:, 0:H3], start=True, stop=False)
                        nc.tensor.matmul(bank[2][:, 0:H3], g2[:], w3[:], start=False, stop=True).then_inc(t3, 1)
                        pe.wait_ge(r3, t + 1)
                        nc.tensor.matmul(bank[3][:, 0:HX], S[:], g3[:], start=True, stop=True).then_inc(t4, 1)
                    with pe.Fori(0, NC) as c:
                        pe.wait_ge(one_ready, c + 1)
                        nc.tensor.transpose(bank[4][0:HX, 0:NP], s_one[:], ident[0:NP, 0:NP]).then_inc(one_tr, 1)

                @gblock.scalar
                def _(act):
                    act.wait_ge(low_set, 3)
                    with act.Fori(0, NT) as t:
                        act.wait_ge(t1, t + 1)
                        nc.scalar.activation(g1[:], bank[0][0:H1, 0:P], ACT.Relu).then_inc(r1, 1)
                        act.wait_ge(t2, t + 1)
                        nc.scalar.activation(g2[:], bank[1][:, 0:P], ACT.Relu, bias=b2c[:]).then_inc(r2, 1)
                        act.wait_ge(t3, t + 1)
                        nc.scalar.activation(g3[:, 0:H3], bank[2][:, 0:H3], ACT.Relu).then_inc(r3, 1)

                @gblock.vector
                def _(dve):
                    LINKS = 7
                    with dve.Fori(0, NT) as t:
                        links = [0]

                        def link(ins):
                            links[0] += 1
                            ins.then_inc(g_chain, 1)
                            dve.wait_ge(g_chain, t * LINKS + links[0])

                        dve.wait_ge(ids_in, t * 48 + 48)
                        nc.vector.tensor_scalar(d_clip[:], d_col[:], float(N - 1), None, ALU.min).then_inc(clip_ready, 1)
                        link(nc.vector.tensor_copy(d_f[:], d_col[:]))
                        link(nc.vector.tensor_scalar(S[:], d_row[:], d_f[:], None, ALU.is_equal))
                        dve.wait_ge(low_set, 3)
                        link(nc.vector.tensor_tensor(S_low[:], S[:], low[:], ALU.mult))
                        link(nc.vector.tensor_reduce(dup[:], S_low[:], AX.X, ALU.add))
                        link(nc.vector.scalar_tensor_tensor(out=d_once[:], in0=dup[:], scalar=float(PAD_DST), in1=d_col[:],
                                                            op0=ALU.mult, op1=ALU.add))
                        dve.wait_ge(rows_in, t * 48 + 48)
                        link(nc.vector.tensor_tensor(z_e[:], B_r[:], A_r[:, 2, :], ALU.add))
                        link(nc.vector.tensor_tensor(z_e[:], z_e[:], A_r[:, 1, :], ALU.add))
                        nc.vector.tensor_tensor(z_e[:], z_e[:], A_r[:, 0, :], ALU.add).then_inc(z_ready, 1)
                        assert links[0] == LINKS
                        dve.wait_ge(t4, t + 1)
                        nc.vector.tensor_tensor(new[:], bank[3][:, 0:HX], old[:], ALU.add).then_inc(new_ready, 1)
                    dve.wait_ge(all_in, 16)
                    with dve.Fori(0, NC) as c:
                        nc.vector.tensor_copy(s_one[:], s_all[:, bass.ds(c, 1), :].rearrange("p c k -> p (c k)")).then_inc(one_ready, 1)
                        dve.wait_ge(one_tr, c + 1)
                        nc.vector.tensor_copy(acc.rearrange("k (p c) -> k c p", c=NC)[:, bass.ds(c, 1), :].rearrange("k c p -> k (c p)"),
                                              bank[4][0:HX, 0:NP]).then_inc(one_done, 1)
                    dve.wait_ge(one_done, NC)

        fin = ExitStack()
        with fin:
            NB = 10
            DX = DO + 1
            part = fin.enter_context(nc.sbuf_tensor("part", [HX, 2, NB, NP], fp32))
            cnt = fin.enter_context(nc.sbuf_tensor("cnt", [NP, 2, NB], fp32))
            o_sb = fin.enter_context(nc.sbuf_tensor("o_sb", [NP, 2, NB * DO], fp32))
            part_ready, y_ready, y_read, o_ready2, n_chain = [
                fin.enter_context(nc.semaphore(n)) for n in ("part_ready", "y_ready", "y_read", "out_ready", "n_chain")]
            o_out = [fin.enter_context(nc.semaphore(f"o_out{i}")) for i in range(2)]
            out_v = out.rearrange("(p c) d -> p (c d)", p=NP)
            nblock = fin.enter_context(nc.Block())
            BATCHES = NC // NB

            def batches(eng, step):
                for n in range(2):
                    step(n, n)
                with eng.Fori(1, BATCHES // 2) as i:
                    for b in range(2):
                        step(i * 2 + b, b)

            @nblock.scalar
            def _(act):
                def step(n, b):
                    unless_zero(act, y_ready, n - 1)
                    nc.scalar.activation(part[:, b, :, :], acc.rearrange("k (p c) -> k c p", c=NC)[:, bass.ds(n * NB, NB), :],
                                         ACT.Copy).then_inc(part_ready, 1)
                batches(act, step)

            @nblock.tensor
            def _(pe):
                def step(n, b):
                    pe.wait_ge(part_ready, n + 1)
                    unless_zero(pe, y_read, n - 1)
                    for c in range(NB):
                        last = nc.tensor.matmul(bank[b][0:NP, c * DX:(c + 1) * DX], part[:, b, c, :], w4[:], start=True, stop=True)
                    last.then_inc(y_ready, 1)
                batches(pe, step)

            @nblock.vector
            def _(dve):
                def step(n, b):
                    y = bank[b][0:NP, 0:NB * DX].rearrange("p (c d) -> p c d", d=DX)
                    o = o_sb[:, b, :].rearrange("p (c d) -> p c d", d=DO)
                    dve.wait_ge(y_ready, n + 1)
                    nc.vector.tensor_scalar(cnt[:, b, :], y[:, :, DO], 1.0, None, ALU.max).then_inc(n_chain, 1)
                    dve.wait_ge(n_chain, n * 2 + 1)
                    nc.vector.reciprocal(cnt[:, b, :], cnt[:, b, :]).then_inc(n_chain, 1)
                    dve.wait_ge(n_chain, n * 2 + 2)
                    unless_zero(dve, o_out[b], (n - b) * 8)
                    nc.vector.tensor_tensor(o, y[:, :, 0:DO], cnt[:, b, :].unsqueeze(2).to_broadcast([NP, NB, DO]),
                                            ALU.mult).then_inc(y_read, 1)
                    dve.wait_ge(y_read, n + 1)
                    nc.vector.tensor_tensor(o_sb[:, b, :], o_sb[:, b, :], x_sb[:, bass.ds(n * (NB * D), NB * D)],
                                            ALU.add).then_inc(o_ready2, 1)
                batches(dve, step)

            @nblock.sync
            def _(sp):
                def step(n, b):
                    sp.wait_ge(o_ready2, n + 1)
                    sp.dma_start(out_v[:, bass.ds(n * (NB * DO), NB * DO)], o_sb[:, b, :]).then_inc(o_out[b], 16)
                batches(sp, step)
                sp.wait_ge(o_out[0], 16 * (BATCHES // 2))
                sp.wait_ge(o_out[1], 16 * (BATCHES // 2))


_INS = ["x", "src", "dst", "L0_gnn_W1", "L0_gnn_b1", "L0_gnn_W2", "L0_gnn_b2", "L0_gnn_W3", "L0_gnn_b3", "L0_gnn_W4", "L0_gnn_b4"]


def kernel(**inputs):
    import numpy as _np
    import concourse.bacc as _bacc
    from concourse import mybir as _mybir
    from concourse.bass_utils import run_bass_kernel_spmd as _run

    nc = _bacc.Bacc("TRN2", target_bir_lowering=False, num_devices=1)
    arrays, args = {}, []
    for name in _INS:
        a = _np.ascontiguousarray(inputs[name])
        arrays[f"in_{name}"] = a
        args.append(nc.dram_tensor(f"in_{name}", a.shape, _mybir.dt.from_np(a.dtype), kind="ExternalInput").ap())
    shape = arrays["in_x"].shape
    args.append(nc.dram_tensor("out_dram", shape, _mybir.dt.float32, kind="ExternalOutput").ap())
    build(nc, *args)
    r = _run(nc, [arrays], core_ids=[0])
    return r.results[0]["out_dram"]
```

```python
import concourse.bass as bass
from concourse import mybir
from concourse.alu_op_type import AluOpType as ALU
from contextlib import ExitStack



def build(nc, x, src, dst, W1, b1, W2, b2, W3, b3, W4, b4, out):
    fp32, bf16, i32 = mybir.dt.float32, mybir.dt.bfloat16, mybir.dt.int32
    ACT = mybir.ActivationFunctionType
    AX = mybir.AxisListType

    P = 128
    N, D = x.shape
    E = src.shape[0]
    H1, H2 = W2.shape
    H3 = W3.shape[1]
    DO = W4.shape[1]
    EPS = 1e-5

    NP, NC = 125, N // 125
    NQ = 4
    PW = 2 * NQ
    PN = -(-NC // PW)
    PB = [0, 2, 5, 8, 11, PN]
    KC = len(PB) - 1
    CB = [min(b * PW, NC) for b in PB]
    CM = max(CB[k + 1] - CB[k] for k in range(KC))

    T = 4
    GE = T * P
    GR = 8
    G = -(-E // GE)
    QP = -(-G // GR)
    GA = QP * GR
    RL = GR * GE
    LAST = E - (QP - 1) * RL
    U = 8
    V = 4
    GP = U - 1
    GL = (G - U) // U
    W = 32
    PAD_DST = 1 << 20
    KA = 3 * W

    NT = -(-E // P)
    HX = H3 + 1

    def dram(name, shape, dt):
        return nc.dram_tensor(name, shape, dt, kind="Internal").ap()

    A_tab = dram("A_tab", (N * 3, H1), bf16)
    B_tab = dram("B_tab", (N, H1), fp32)
    base_tab = dram("base_tab", (GA,), i32)
    sum_tab = dram("sum_tab", (N, HX), fp32)

    ctx = ExitStack()
    with ctx:
        def sb(name, shape, dt=fp32):
            return ctx.enter_context(nc.sbuf_tensor(name, shape, dt))

        def sem(name):
            return ctx.enter_context(nc.semaphore(name))

        bank = [ctx.enter_context(nc.psum_tensor(f"bank{i}", [P, 512], fp32)) for i in range(8)]

        x_sb = sb("x_sb", [NP, NC * D])
        big = sb("big", [P, N])
        cen = big[0:NP, 0:NC * D]
        src_raw = big[0:QP, NC * D:NC * D + RL]
        dst_raw = big[0:QP, NC * D + RL:NC * D + 2 * RL]
        acc = big[0:HX, :]
        src_T = sb("src_T", [P, GA, T], i32)
        rel_T = sb("rel_T", [P, GA, T])
        base_bc = sb("base_bc", [P, GA], i32)
        base_row = sb("base_row", [1, GA], i32)
        ident = sb("ident", [P, P])
        iota_w = sb("iota_w", [P, T, W, 3])
        zeros = sb("zeros", [HX, 500])
        w2 = sb("w2", [H1, H2])
        w3 = sb("w3", [H2, H3])
        w4 = sb("w4", [HX, DO + 1])
        b2c = sb("b2c", [H2, 1])
        b_row = sb("b_row", [1, 2, H3])
        b_r = sb("b_r", [1, 2, H3])
        b_p = sb("b_p", [1, 3, 2, H3], bf16)
        A_p = sb("A_p", [NP, NC, 3, H1], bf16)
        b_k = sb("b_k", [3, 2, H3], bf16)
        ones_b = sb("ones_b", [3, P], bf16)
        eps_c = sb("eps_c", [P, 1])
        flag_i = sb("flag_i", [1, 1], i32)
        idx = sb("idx", [P, U, T], i32)
        B_g = sb("B_g", [P, U, T, H1])

        x_in = [sem(f"x_in{k}") for k in range(KC)]
        src_in, dst_in, w_in, w2_in = sem("src_in"), sem("dst_in"), sem("w_in"), sem("w2_in")
        w1a_in = sem("w1a_in")
        b_in_sem = sem("bias_in")
        pool_const, pads_set, iota_ready, iota_mid = sem("pool_const"), sem("pads_set"), sem("iota_ready"), sem("iota_mid")
        dch = sem("dch")
        eps_ready, mean_ready, cen_ready, sq_ready = sem("eps_ready"), sem("mean_ready"), sem("cen_ready"), sem("sq_ready")
        ssq_ready, sd_ready, h_ready = sem("ssq_ready"), sem("sd_ready"), sem("h_ready")
        bdB_ready, bdA_ready = sem("bdB_ready"), sem("bdA_ready")
        src_fp, dst_fp, idx_tr, src_cp, dst_cp = sem("src_fp"), sem("dst_fp"), sem("idx_tr"), sem("src_cp"), sem("dst_cp")
        hT_tr, hT_cp, tabB_mm, tabB_cp, tabA_mm = sem("hT_tr"), sem("hT_cp"), sem("tabB_mm"), sem("tabB_cp"), sem("tabA_mm")
        BS = 3
        B_out = [sem(f"B_out{i}") for i in range(BS)]
        A_hi, A_rest, A_mid, A_lo, A_out = sem("A_hi"), sem("A_rest"), sem("A_mid"), sem("A_lo"), sem("A_out")
        base_ready, base_out, base_in, baseb_in = sem("base_ready"), sem("base_out"), sem("base_in"), sem("baseb_in")
        bad_ready, bad_mm, flag_ready = sem("bad_ready"), sem("bad_mm"), sem("flag_ready")
        b_ready, bk_in = sem("b_ready"), sem("bk_in")
        acc_zero, zero_set = sem("acc_zero"), sem("zero_set")
        idx_ready, turn = sem("idx_ready"), sem("turn")
        b_in = [sem(f"b_in{u}") for u in range(U)]

        def ids(g, u):
            nc.scalar.activation(idx[:, u, :], src_T[:, bass.ds(g, 1), :].rearrange("p g j -> p (g j)"),
                                 ACT.Copy).then_inc(idx_ready, 1)

        def tiles(g):
            return min(T, NT - g * T) if isinstance(g, int) else T

        def gather(pool, g, u):
            pool.wait_ge(idx_ready, g + 1)
            pool.sem_inc(turn, 1)
            for j in range(tiles(g)):
                nc.gpsimd.indirect_dma_start(
                    out=B_g[:, u, j, :], out_offset=None, in_=B_tab[:, :],
                    in_offset=bass.IndirectOffsetOnAxis(ap=idx[:, u, j:j + 1], axis=0)).then_inc(b_in[u], 16)

        prep = ExitStack()
        with prep:
            def psb(name, shape, dt=fp32):
                return prep.enter_context(nc.sbuf_tensor(name, shape, dt))

            sq = psb("sq", [NP, NC * D])
            st = psb("st", [NP, 4, NC])
            hT = psb("hT", [P, NC // NQ, NP])
            B_sb = psb("B_sb", [NP, BS, CM, H1])
            RS = 5
            A_r = psb("A_r", [NP, RS, PW, H1])
            w1a = psb("w1a", [P, H1])
            w1b = psb("w1b", [P, H1])
            w1_bd = psb("w1_bd", [P, 2, NQ, H1])
            base_i = psb("base_i", [QP, GR], i32)
            far = psb("far", [P, 2])
            bad = psb("bad", [P, 1])
            ones_f = psb("ones_f", [P, 1])
            tabl = psb("tabl", [1, 1])
            src_i = src_raw.bitcast(i32)
            dst_i = dst_raw.bitcast(i32)
            RH = RL // 2
            R0 = 4
            ZC = 2500

            def cols(t, k):
                return t[:, CB[k] * D:CB[k + 1] * D].rearrange("p (c d) -> p c d", d=D)

            def spread(t, k):
                return t[:, CB[k]:CB[k + 1]].unsqueeze(2).to_broadcast([NP, CB[k + 1] - CB[k], D])

            def pair(n):
                return slice(n * PW, min(n * PW + PW, NC))

            def quads(n):
                return range(2 * n, min(2 * n + 2, NC // NQ))

            def chunk_of(n):
                return max(k for k in range(KC) if PB[k] <= n)

            block = prep.enter_context(nc.Block(no_gpsimd_drain=True))
            hT_ps, B_ps = bank[2:4], bank[6:8]
            A_ps = bank[4:6] + bank[2:4]

            @block.gpsimd
            def _(pool):
                pad0 = (QP - 1) // 32 * 32
                nc.gpsimd.memset(src_i[pad0:QP, LAST:RL], 0).then_inc(pads_set, 1)
                nc.gpsimd.memset(dst_i[pad0:QP, LAST:RL], PAD_DST).then_inc(pads_set, 1)
                pool.wait_ge(pads_set, 2)
                nc.gpsimd.memset(ident[:], 0.0).then_inc(pool_const, 1)
                pool.wait_ge(pool_const, 1)
                nc.gpsimd.affine_select(out=ident[:], in_=ident[:], compare_op=ALU.not_equal, fill=1.0, base=0,
                                        pattern=[[-1, P]], channel_multiplier=1).then_inc(pool_const, 1)
                nc.gpsimd.memset(ones_b[:], 1.0).then_inc(pool_const, 1)
                nc.gpsimd.memset(ones_f[:], 1.0).then_inc(pool_const, 1)
                for k in range(KC):
                    pool.wait_ge(mean_ready, k + 1)
                    nc.gpsimd.tensor_tensor(cols(cen, k), cols(x_sb, k), spread(st[:, 1, :], k), ALU.add).then_inc(cen_ready, 1)
                nc.gpsimd.iota(iota_w[:], pattern=[[0, T], [1, W], [0, 3]], base=0, channel_multiplier=0,
                               allow_small_or_imprecise_dtypes=True).then_inc(iota_ready, 1)
                nc.gpsimd.memset(zeros[:], 0.0).then_inc(zero_set, 1)
                for b in range(BS):
                    pool.wait_ge(B_out[b], 16 * len(range(b, KC, BS)))
                for g in range(GP):
                    gather(pool, g, g)

            @block.sync
            def _(sp):
                def load_x(k):
                    sp.dma_start(cols(x_sb, k).rearrange("p c d -> p (c d)"),
                                 x.rearrange("(p c) d -> p (c d)", p=NP)[:, CB[k] * D:CB[k + 1] * D]).then_inc(x_in[k], 16)

                def load_ids(raw, arr, s):
                    sp.dma_start(raw[0:QP - 1, :], arr[0:(QP - 1) * RL].rearrange("(q e) -> q e", e=RL)).then_inc(s, 16)
                    sp.dma_start(raw[QP - 1:QP, 0:LAST], arr[(QP - 1) * RL:E].rearrange("(q e) -> q e", q=1)).then_inc(s, 16)

                load_x(0)
                load_x(1)
                sp.wait_ge(pads_set, 2)
                load_ids(src_i, src, src_in)
                for k in range(2, KC):
                    load_x(k)
                load_ids(dst_i, dst, dst_in)
                sp.dma_start(b_row[:, 0, :], b3.rearrange("(o d) -> o d", o=1)).then_inc(b_in_sem, 16)
                sp.dma_start(b_row[:, 1, :], b1.rearrange("(o d) -> o d", o=1)).then_inc(b_in_sem, 16)
                for c in range(NQ):
                    sp.dma_start(w1a[c * D:(c + 1) * D, :], W1[0:D, :]).then_inc(w1a_in, 16)
                sp.dma_start(w2[:], W2).then_inc(w2_in, 16)
                sp.dma_start(w3[:], W3).then_inc(w2_in, 16)
                sp.dma_start(w4[0:H3, 0:DO], W4).then_inc(w2_in, 16)
                sp.dma_start(w4[H3:HX, 0:DO], b4.rearrange("(o d) -> o d", o=1)).then_inc(w2_in, 16)
                sp.dma_start(b2c[:], b2.rearrange("(d o) -> d o", o=1)).then_inc(w2_in, 16)
                sp.wait_ge(b_ready, 1)
                for k in range(3):
                    sp.dma_start(b_k[k:k + 1, :, :], b_p[:, k, :, :]).then_inc(bk_in, 16)
                Bv = B_tab.rearrange("(p c) d -> p c d", p=NP)
                for k in range(KC):
                    sp.wait_ge(tabB_cp, PB[k + 1])
                    sp.dma_start(Bv[:, CB[k]:CB[k + 1], :], B_sb[:, k % BS, 0:CB[k + 1] - CB[k], :]).then_inc(B_out[k % BS], 16)
                sp.wait_ge(base_ready, 1)
                sp.dma_start(base_tab.rearrange("(q r) -> q r", r=GR), base_i[:]).then_inc(base_out, 16)
                sp.wait_ge(base_out, 16)
                sp.dma_start(base_bc[:], base_tab.partition_broadcast(P)).then_inc(baseb_in, 16)
                sp.dma_start(base_row[:], base_tab.rearrange("(o g) -> o g", o=1)).then_inc(base_in, 16)
                sp.wait_ge(zero_set, 1)
                sp.wait_ge(hT_tr, PN)
                sp.wait_ge(idx_tr, GR)
                behind_src = (NC * D + RL) // ZC * ZC
                behind_dst = -(-(NC * D + 2 * RL) // ZC) * ZC

                def zero(c0, c1):
                    for c in range(c0, c1, ZC):
                        sp.dma_start(acc[:, c:c + ZC].rearrange("p (a b) -> p a b", b=500),
                                     zeros[:].unsqueeze(1).to_broadcast([HX, ZC // 500, 500])).then_inc(acc_zero, 16)

                zero(0, behind_src)
                zero(behind_dst, N)
                Av = A_tab.rearrange("(p c k) d -> p c k d", p=NP, k=3)
                for k in range(KC):
                    sp.wait_ge(A_lo, PB[k + 1])
                    sp.dma_start(Av[:, CB[k]:CB[k + 1], :, :], A_p[:, CB[k]:CB[k + 1], :, :]).then_inc(A_out, 16)
                sp.wait_ge(idx_tr, 2 * GR)
                zero(behind_src, behind_dst)
                sp.wait_ge(base_in, 16)
                sp.wait_ge(w2_in, 16 * 5)

            @block.scalar
            def _(act):
                act.wait_ge(eps_ready, 1)
                nc.scalar.activation(tabl[:], eps_c[0:1, :], ACT.Sqrt)
                for c in range(NQ):
                    act.dma_start(w1b[c * D:(c + 1) * D, :], W1[D:2 * D, :]).then_inc(w_in, 16)

                def square(k):
                    act.wait_ge(cen_ready, k + 1)
                    nc.scalar.activation(cols(sq, k), cols(cen, k), ACT.Square).then_inc(sq_ready, 1)

                def deviation(k):
                    act.wait_ge(ssq_ready, k + 1)
                    nc.scalar.activation(st[:, 3, CB[k]:CB[k + 1]], st[:, 2, CB[k]:CB[k + 1]], ACT.Sqrt,
                                         bias=eps_c[0:NP, :], scale=1.0 / D).then_inc(sd_ready, 1)

                def table_B(n):
                    if n < PN:
                        act.wait_ge(hT_tr, n + 1)
                        q = quads(n)
                        nc.scalar.activation(hT[:, q[0]:q[-1] + 1, :].rearrange("p q n -> p (q n)"), hT_ps[n % 2][:, 0:len(q) * NP],
                                             ACT.Copy).then_inc(hT_cp, 1)
                    m = n - 1
                    if m >= 0:
                        k = chunk_of(m)
                        c0, c1 = pair(m).start - CB[k], pair(m).stop - CB[k]
                        act.wait_ge(tabB_mm, m + 1)
                        if m == PB[k] and k >= BS:
                            act.wait_ge(B_out[k % BS], 16 * (k // BS))
                        nc.scalar.activation(B_sb[:, k % BS, c0:c1, :],
                                             B_ps[m % 2][0:NP, 0:(c1 - c0) * H1].rearrange("p (c w) -> p c w", w=H1),
                                             ACT.Copy).then_inc(tabB_cp, 1)
                    r = n - R0
                    if 0 <= r < GR:
                        act.wait_ge(idx_tr, r + 1)
                        nc.scalar.activation(src_T[:, :, :].rearrange("p (q r) j -> p r j q", r=GR)[:, r, :, :],
                                             bank[r % 2][:, 0:T * QP].rearrange("p (j q) -> p j q", j=T), ACT.Copy).then_inc(src_cp, 1)

                square(0)
                for k in range(KC):
                    if k + 1 < KC:
                        square(k + 1)
                    deviation(k)
                    if k in (1, 2):
                        act.wait_ge(src_in, 32)
                        half = slice((k - 1) * RH, k * RH)
                        nc.scalar.activation(src_raw[:, half], src_i[:, half], ACT.Copy).then_inc(src_fp, 1)
                    if k >= 1:
                        for n in range(PB[k - 1], PB[k]):
                            table_B(n)
                for n in range(PB[KC - 1], PN + 1):
                    table_B(n)
                act.wait_ge(src_cp, GR)
                nc.scalar.activation(idx[:], src_T[:, 0:U, :], ACT.Copy).then_inc(idx_ready, U)
                act.wait_ge(dst_in, 32)
                act.wait_ge(base_ready, 1)
                nc.scalar.activation(dst_raw[:, RH:], dst_i[:, RH:], ACT.Copy).then_inc(dst_fp, 1)
                for n in range(PN + 2):
                    if n < PN:
                        c = pair(n)
                        act.wait_ge(tabA_mm, n + 1)
                        nc.scalar.activation(A_p[:, c, 0, :], A_ps[n % 4][0:NP, 0:(c.stop - c.start) * H1].rearrange("p (c w) -> p c w", w=H1),
                                             ACT.Copy).then_inc(A_hi, 1)
                    m = n - 2
                    if m >= 0:
                        c = pair(m)
                        act.wait_ge(A_rest, m + 1)
                        nc.scalar.activation(A_p[:, c, 1, :], A_r[:, m % RS, 0:c.stop - c.start, :], ACT.Copy).then_inc(A_mid, 1)

            @block.tensor
            def _(pe):
                def index_rows(n, raw):
                    r = n % GR
                    if 2 <= n < GR + 2:
                        pe.wait_ge(src_cp, n - 1)
                    elif n >= GR + 2:
                        pe.wait_ge(dst_cp, n - GR - 1)
                    for j in range(T):
                        last = nc.tensor.transpose(bank[n % 2][:, j * QP:(j + 1) * QP],
                                                   raw[:, r * GE + j * P:r * GE + (j + 1) * P], ident[0:QP, 0:QP])
                    last.then_inc(idx_tr, 1)

                pe.wait_ge(pool_const, 4)
                pe.wait_ge(bdB_ready, 1)
                for n in range(PN + 1):
                    if n < PN:
                        pe.wait_ge(h_ready, chunk_of(n) + 1)
                        if n >= 2:
                            pe.wait_ge(hT_cp, n - 1)
                        for i, q in enumerate(quads(n)):
                            last = nc.tensor.transpose(hT_ps[n % 2][:, i * NP:(i + 1) * NP], cen[:, q * NQ * D:(q + 1) * NQ * D],
                                                       ident[0:NP, 0:NP])
                        last.then_inc(hT_tr, 1)
                    m = n - 1
                    if m >= 0:
                        pe.wait_ge(hT_cp, m + 1)
                        if m >= 2:
                            pe.wait_ge(tabB_cp, m - 1)
                        for i, q in enumerate(quads(m)):
                            last = nc.tensor.matmul(B_ps[m % 2][0:NP, i * NQ * H1:(i + 1) * NQ * H1], hT[:, q, :],
                                                    w1_bd[:, 1, :, :].rearrange("p c w -> p (c w)"), start=True, stop=True)
                        last.then_inc(tabB_mm, 1)
                    r = n - R0
                    if 0 <= r < GR:
                        pe.wait_ge(src_fp, 1 + (r >= GR // 2))
                        index_rows(r, src_raw)
                pe.wait_ge(bk_in, 48)
                pe.wait_ge(bdA_ready, 1)
                for n in range(max(PN, GR + 5)):
                    if n < PN:
                        if n >= 4:
                            pe.wait_ge(A_rest, n - 3)
                        w = (pair(n).stop - pair(n).start) * H1
                        nc.tensor.matmul(A_ps[n % 4][0:NP, 0:w], ones_b[:, 0:NP], b_k[:, 1:2, :].to_broadcast([3, w // H1, H1]), start=True, stop=False)
                        for i, q in enumerate(quads(n)):
                            last = nc.tensor.matmul(A_ps[n % 4][0:NP, i * NQ * H1:(i + 1) * NQ * H1], hT[:, q, :],
                                                    w1_bd[:, 0, :, :].rearrange("p c w -> p (c w)"), start=False, stop=(q == quads(n)[-1]))
                        last.then_inc(tabA_mm, 1)
                    r = n - 5
                    if 0 <= r < GR:
                        pe.wait_ge(dst_fp, 2)
                        index_rows(GR + r, dst_raw)
                pe.wait_ge(bad_ready, 1)
                pe.wait_ge(tabB_cp, PN)
                nc.tensor.matmul(bank[7][0:1, 0:1], bad[:], ones_f[:], start=True, stop=True).then_inc(bad_mm, 1)

            @block.vector
            def _(dve):
                chain = [0]

                def link(ins):
                    chain[0] += 1
                    ins.then_inc(dch, 1)
                    dve.wait_ge(dch, chain[0])

                def mean(k):
                    c = slice(CB[k], CB[k + 1])
                    dve.wait_ge(x_in[k], 16)
                    link(nc.vector.tensor_reduce(st[:, 0, c], cols(x_sb, k), AX.X, ALU.add))
                    nc.vector.tensor_scalar(st[:, 1, c], st[:, 0, c], -1.0 / D, None, ALU.mult).then_inc(mean_ready, 1)

                def normalise(k):
                    c = slice(CB[k], CB[k + 1])
                    dve.wait_ge(sq_ready, k + 1)
                    nc.vector.tensor_reduce(st[:, 2, c], cols(sq, k), AX.X, ALU.add).then_inc(ssq_ready, 1)
                    dve.wait_ge(sd_ready, k + 1)
                    link(nc.vector.reciprocal(st[:, 3, c], st[:, 3, c]))
                    nc.vector.scalar_tensor_tensor(out=cols(cen, k), in0=cols(cen, k), scalar=0.0, in1=spread(st[:, 3, :], k),
                                                   op0=ALU.max, op1=ALU.mult).then_inc(h_ready, 1)

                nc.vector.memset(eps_c[:], EPS).then_inc(eps_ready, 1)
                nc.vector.memset(w4[0:H3, DO:DO + 1], 0.0)
                nc.vector.memset(w4[H3:HX, DO:DO + 1], 1.0)
                nc.vector.memset(far[:], 0.0)
                link(nc.vector.memset(w1_bd[:], 0.0))
                mean(0)
                mean(1)
                for k in range(KC):
                    if k == 1:
                        dve.wait_ge(w_in, 16 * NQ)
                        for c in range(NQ):
                            rows = slice(c * D, (c + 1) * D)
                            last = nc.vector.tensor_copy(w1_bd[rows, 1, c, :], w1b[rows, :])
                        last.then_inc(bdB_ready, 1)
                    if k == 2:
                        dve.wait_ge(b_in_sem, 32)
                        link(nc.vector.tensor_copy(b_p[:, 0, :, :], b_row[:]))
                        link(nc.vector.tensor_tensor(b_r[:], b_row[:], b_p[:, 0, :, :], ALU.subtract))
                        link(nc.vector.tensor_copy(b_p[:, 1, :, :], b_r[:]))
                        nc.vector.tensor_tensor(b_p[:, 2, :, :], b_r[:], b_p[:, 1, :, :], ALU.subtract).then_inc(b_ready, 1)
                    normalise(k)
                    if k + 2 < KC:
                        mean(k + 2)
                dve.wait_ge(dst_in, 32)
                nc.vector.tensor_scalar(base_i[:], dst_i.rearrange("q (r e) -> q r e", e=GE)[:, :, 0], float(N - W), None,
                                        ALU.min).then_inc(base_ready, 1)
                dve.wait_ge(w1a_in, 16 * NQ)
                for c in range(NQ):
                    rows = slice(c * D, (c + 1) * D)
                    last = nc.vector.tensor_tensor(w1_bd[rows, 0, c, :], w1a[rows, :], w1b[rows, :], ALU.subtract)
                last.then_inc(bdA_ready, 1)
                dve.wait_ge(base_ready, 1)
                nc.vector.tensor_copy(dst_raw[:, 0:RH], dst_i[:, 0:RH]).then_inc(dst_fp, 1)
                dve.wait_ge(iota_ready, 1)
                nc.vector.tensor_scalar(iota_w[:], iota_w[:], -(W - 1) / 2, None, ALU.add).then_inc(iota_mid, 1)
                for n in range(PN + 3):
                    if n < PN:
                        c = pair(n)
                        w = c.stop - c.start
                        dve.wait_ge(A_hi, n + 1)
                        if n >= RS:
                            dve.wait_ge(A_lo, n - RS + 1)
                        nc.vector.tensor_tensor(A_r[:, n % RS, 0:w, :], A_ps[n % 4][0:NP, 0:w * H1].rearrange("p (c w) -> p c w", w=H1),
                                                A_p[:, c, 0, :], ALU.subtract).then_inc(A_rest, 1)
                    m = n - 3
                    if m >= 0:
                        c = pair(m)
                        dve.wait_ge(A_mid, m + 1)
                        nc.vector.tensor_tensor(A_p[:, c, 2, :], A_r[:, m % RS, 0:c.stop - c.start, :], A_p[:, c, 1, :],
                                                ALU.subtract).then_inc(A_lo, 1)
                    r = n - 4
                    if 0 <= r < GR:
                        if r == 0:
                            dve.wait_ge(baseb_in, 16)
                        dve.wait_ge(idx_tr, GR + r + 1)
                        nc.vector.scalar_tensor_tensor(out=rel_T[:, :, :].rearrange("p (q r) j -> p r j q", r=GR)[:, r, :, :],
                                                       in0=bank[r % 2][:, 0:T * QP].rearrange("p (j q) -> p j q", j=T),
                                                       scalar=-(W - 1) / 2,
                                                       in1=base_bc[:].rearrange("p (q r) -> p r q", r=GR)[:, r, :].unsqueeze(1).to_broadcast([P, T, QP]),
                                                       op0=ALU.add, op1=ALU.subtract).then_inc(dst_cp, 1)
                rel = rel_T[:, :, :].rearrange("p g j -> p (g j)")
                full, part = E // P, E % P
                dve.wait_ge(dst_cp, GR)
                link(nc.vector.tensor_reduce(far[:, 0:1], rel[:, 0:full], AX.X, ALU.max, apply_absolute_value=True))
                if part:
                    link(nc.vector.tensor_reduce(far[0:part, 1:2], rel[0:part, full:full + 1], AX.X, ALU.max,
                                                 apply_absolute_value=True))
                link(nc.vector.tensor_scalar(far[:], far[:], W / 2, None, ALU.is_ge))
                nc.vector.tensor_tensor(bad[:], far[:, 0:1], far[:, 1:2], ALU.max).then_inc(bad_ready, 1)
                dve.wait_ge(bad_mm, 1)
                nc.vector.tensor_copy(flag_i[:], bank[7][0:1, 0:1]).then_inc(flag_ready, 1)
                dve.wait_ge(iota_mid, 1)
                dve.wait_ge(flag_ready, 1)

        flag = nc.values_load(flag_i[0:1, 0:1], min_val=0, max_val=P)

        def unless_zero(eng, s, count):
            if not isinstance(count, int) or count > 0:
                eng.wait_ge(s, count)

        with nc.If(flag == 0):
            fast = ExitStack()
            with fast:
                def fsb(name, shape, dt=fp32):
                    return fast.enter_context(nc.sbuf_tensor(name, shape, dt))

                def fsem(name):
                    return fast.enter_context(nc.semaphore(name))

                A_w = fsb("A_w", [KA, U, H1], bf16)
                O = fsb("O", [P, V, T, W, 3])
                OT = fsb("OT", [KA, 2, GE], bf16)
                h1 = fsb("h1", [H1, 2, GE])
                h2 = fsb("h2", [H2, 2, GE])
                h3 = fsb("h3", [P, 2, T, HX])
                z1, z2, z3 = bank[0:2], bank[2:4], bank[4:6]
                ot_ps = bank[6]
                seg = bank[7]

                a_in = [fsem(f"a_in{u}") for u in range(U)]
                ones_set = fsem("ones_set")
                o_ready, ot_ready, otc_ready = fsem("o_ready"), fsem("ot_ready"), fsem("otc_ready")
                z1_ready, behind_dstready, z3_ready, seg_ready = fsem("z1_ready"), fsem("behind_dstready"), fsem("z3_ready"), fsem("seg_ready")
                h1_ready, h2_ready, h3_ready, acc_done = fsem("h1_ready"), fsem("h2_ready"), fsem("h3_ready"), fsem("acc_done")

                def live(g):
                    return not isinstance(g, int) or 0 <= g < G

                def groups(eng, step, first=0, after=0):
                    for g in range(first, U):
                        step(g, g % U)
                    with eng.Fori(1, GL) as i:
                        for u in range(U):
                            step(i * U + u, u)
                    for g in range(GL * U, G + after):
                        step(g, g % U)

                fblock = fast.enter_context(nc.Block())

                @fblock.sync
                def _(sp):
                    def step(g, u):
                        unless_zero(sp, z1_ready, g - U + 1)
                        first = sp.value_load(base_row[0:1, bass.ds(g, 1)], min_val=0, max_val=N - W)
                        sp.dma_start(A_w[:, u, :], A_tab[bass.ds(first * 3, KA), :]).then_inc(a_in[u], 16)
                    sp.wait_ge(A_out, 16 * KC)
                    groups(sp, step)

                @fblock.gpsimd
                def _(pool):
                    groups(pool, lambda g, u: gather(pool, g, u), first=GP)

                @fblock.tensor
                def _(pe):
                    def step(g, u):
                        if live(g - 3):
                            s, b = (u - 3) % V, (u - 3) % 2
                            pe.wait_ge(h3_ready, g - 2)
                            unless_zero(pe, acc_done, g - 3)
                            for j in range(T):
                                last = nc.tensor.matmul(seg[0:HX, 0:W], h3[:, b, j, :], O[:, s, j, :, 0],
                                                        start=(j == 0), stop=(j == T - 1))
                            last.then_inc(seg_ready, 1)
                        if live(g - 2):
                            b = (u - 2) % 2
                            pe.wait_ge(h2_ready, g - 1)
                            unless_zero(pe, h3_ready, g - 3)
                            nc.tensor.matmul(z3[b][:, 0:T * H3], ones_b[:], b_k[:, 0:1, :].to_broadcast([3, T, H3]), start=True, stop=False)
                            for j in range(T):
                                last = nc.tensor.matmul(z3[b][:, j * H3:(j + 1) * H3], h2[:, b, j * P:(j + 1) * P], w3[:],
                                                        start=False, stop=(j == T - 1))
                            last.then_inc(z3_ready, 1)
                        if live(g - 1):
                            b = (u - 1) % 2
                            pe.wait_ge(h1_ready, g)
                            unless_zero(pe, h2_ready, g - 2)
                            nc.tensor.matmul(z2[b][:, :], w2[:], h1[:, b, :], start=True, stop=True).then_inc(behind_dstready, 1)
                        if live(g):
                            b = u % 2
                            pe.wait_ge(otc_ready, g + 1)
                            pe.wait_ge(a_in[u], (g - u) * (16 // U) + 16)
                            unless_zero(pe, h1_ready, g - 1)
                            nc.tensor.matmul(z1[b][0:H1, :], A_w[:, u, :], OT[:, b, :], start=True, stop=False)
                            pe.wait_ge(b_in[u], (g - u) * (16 * T // U) + 16 * tiles(g))
                            for j in range(T):
                                last = nc.tensor.matmul(z1[b][0:H1, j * P:(j + 1) * P], B_g[:, u, j, :], ident[:],
                                                        start=False, stop=(j == T - 1))
                            last.then_inc(z1_ready, 1)
                        if live(g + 1):
                            s = (u + 1) % V
                            pe.wait_ge(o_ready, g + 2)
                            unless_zero(pe, otc_ready, g + 1)
                            for j in range(T):
                                last = nc.tensor.transpose(ot_ps[0:KA, j * P:(j + 1) * P],
                                                           O[:, s, j, :, :].rearrange("p w k -> p (w k)"), ident[:])
                            last.then_inc(ot_ready, 1)
                    groups(pe, step, first=-1, after=3)

                @fblock.scalar
                def _(act):
                    def step(g, u):
                        if live(g - 2):
                            b = (u - 2) % 2
                            act.wait_ge(z3_ready, g - 1)
                            if isinstance(g, int) and g == 2:
                                act.wait_ge(ones_set, 1)
                            unless_zero(act, seg_ready, g - 3)
                            nc.scalar.activation(h3[:, b, :, 0:H3], z3[b][:, 0:T * H3].rearrange("p (j d) -> p j d", j=T),
                                                 ACT.Relu).then_inc(h3_ready, 1)
                        if live(g - 1):
                            b = (u - 1) % 2
                            act.wait_ge(behind_dstready, g)
                            unless_zero(act, z3_ready, g - 2)
                            nc.scalar.activation(h2[:, b, :], z2[b][:, :], ACT.Relu, bias=b2c[:]).then_inc(h2_ready, 1)
                        if live(g):
                            b = u % 2
                            act.wait_ge(z1_ready, g + 1)
                            unless_zero(act, behind_dstready, g - 1)
                            nc.scalar.activation(h1[:, b, :], z1[b][0:H1, :], ACT.Relu).then_inc(h1_ready, 1)
                            if live(g + U):
                                ids(g + U, u)
                    groups(act, step, after=2)

                @fblock.vector
                def _(dve):
                    nc.vector.memset(h3[:], 1.0).then_inc(ones_set, 1)
                    dve.wait_ge(acc_zero, 16 * (N // ZC))

                    def step(g, u):
                        if live(g - 3):
                            dve.wait_ge(seg_ready, g - 2)
                            unless_zero(dve, acc_done, g - 3)
                            first = dve.value_load(base_row[0:1, bass.ds(g - 3, 1)], min_val=0, max_val=N - W)
                            nc.vector.tensor_tensor(acc[:, bass.ds(first, W)], seg[0:HX, 0:W], acc[:, bass.ds(first, W)],
                                                    ALU.add).then_inc(acc_done, 1)
                        if live(g + 1):
                            s, b = (u + 1) % V, (u + 1) % 2
                            nc.vector.tensor_tensor(O[:, s, :, :, :].rearrange("p j w k -> p j (w k)"),
                                                    rel_T[:, bass.ds(g + 1, 1), :].rearrange("p g j -> p (g j)").unsqueeze(2).to_broadcast([P, T, KA]),
                                                    iota_w[:].rearrange("p j w k -> p j (w k)"), ALU.is_equal).then_inc(o_ready, 1)
                            dve.wait_ge(ot_ready, g + 2)
                            unless_zero(dve, z1_ready, g)
                            nc.vector.tensor_copy(OT[:, b, :], ot_ps[0:KA, :]).then_inc(otc_ready, 1)
                    groups(dve, step, first=-1, after=3)
                    dve.wait_ge(acc_done, G)

        with nc.Else():
            gen = ExitStack()
            with gen:
                def gsb(name, shape, dt=fp32):
                    return gen.enter_context(nc.sbuf_tensor(name, shape, dt))

                def gsem(name):
                    return gen.enter_context(nc.semaphore(name))

                s_col = gsb("s_col", [P, 1], i32)
                d_col = gsb("d_col", [P, 1], i32)
                d_row = gsb("d_row", [P, P], i32)
                d_clip = gsb("d_clip", [P, 1], i32)
                d_f = gsb("d_f", [P, 1])
                S = gsb("S", [P, P])
                S_low = gsb("S_low", [P, P])
                low = gsb("low", [P, P])
                dup = gsb("dup", [P, 1])
                d_once = gsb("d_once", [P, 1], i32)
                B_r = gsb("B_r", [P, H1])
                A_r = gsb("A_r2", [P, 3, H1], bf16)
                z_e = gsb("z_e", [P, H1])
                g1 = gsb("g1", [H1, P])
                g2 = gsb("g2", [H2, P])
                g3 = gsb("g3", [P, HX])
                old = gsb("old", [P, HX])
                new = gsb("new", [P, HX])
                s_all = gsb("s_all", [NP, NC, HX])
                s_one = gsb("s_one", [NP, HX])

                g_turn, pad_ready = gsem("g_turn"), gsem("pad_ready")
                low_set, tab_zero, ids_in, clip_ready, rows_in, g_chain = (
                    gsem("low_set"), gsem("tab_zero"), gsem("ids_in"), gsem("clip_ready"), gsem("rows_in"), gsem("g_chain"))
                z_ready, t1, r1, t2, r2, t3, r3, t4 = [gsem(n) for n in ("z_ready", "t1", "r1", "t2", "r2", "t3", "r3", "t4")]
                new_ready, stored, all_in, one_ready, one_tr, one_done = [
                    gsem(n) for n in ("new_ready", "stored", "all_in", "one_ready", "one_tr", "one_done")]
                A_rows = A_tab.rearrange("(n k) d -> n (k d)", k=3)

                gblock = gen.enter_context(nc.Block())

                @gblock.sync
                def _(sp):
                    sp.dma_start(sum_tab.rearrange("n k -> (n k)").rearrange("(p a b) -> p a b", p=HX, b=500),
                                 zeros[:].unsqueeze(1).to_broadcast([HX, N // 500, 500])).then_inc(tab_zero, 16)

                    def step(t, n):
                        sp.wait_ge(stored, t * 16)
                        sp.dma_start(s_col[0:n, :], src[bass.ds(t * P, n)].rearrange("(p o) -> p o", o=1)).then_inc(ids_in, 16)
                        sp.dma_start(d_col[0:n, :], dst[bass.ds(t * P, n)].rearrange("(p o) -> p o", o=1)).then_inc(ids_in, 16)
                        sp.dma_start(d_row[:, 0:n], dst[bass.ds(t * P, n)].partition_broadcast(P)).then_inc(ids_in, 16)

                    with sp.Fori(0, NT - 1) as t:
                        step(t, P)
                    sp.wait_ge(pad_ready, 2)
                    step(NT - 1, E - (NT - 1) * P)
                    sp.wait_ge(stored, NT * 16)
                    sp.dma_start(s_all[:], sum_tab.rearrange("(p c) k -> p c k", p=NP)).then_inc(all_in, 16)

                @gblock.gpsimd
                def _(pool):
                    nc.gpsimd.memset(low[:], 1.0).then_inc(low_set, 1)
                    pool.wait_ge(low_set, 1)
                    nc.gpsimd.affine_select(out=low[:], in_=low[:], compare_op=ALU.is_gt, fill=0.0, base=0,
                                            pattern=[[-1, P]], channel_multiplier=1).then_inc(low_set, 1)
                    nc.gpsimd.memset(g3[:], 1.0).then_inc(low_set, 1)
                    pool.wait_ge(A_out, 16 * KC)
                    with pool.Fori(0, NT) as t:
                        pool.wait_ge(clip_ready, t + 1)
                        pool.wait_ge(tab_zero, 16)
                        pool.sem_inc(g_turn, 1)
                        for o, tab, i in ((B_r[:, :], B_tab[:, :], s_col), (A_r[:].rearrange("p k d -> p (k d)"), A_rows[:, :], d_clip),
                                          (old[:, :], sum_tab[:, :], d_clip)):
                            nc.gpsimd.indirect_dma_start(out=o, out_offset=None, in_=tab,
                                                         in_offset=bass.IndirectOffsetOnAxis(ap=i[:, 0:1], axis=0)).then_inc(rows_in, 16)
                        pool.wait_ge(new_ready, t + 1)
                        pool.sem_inc(g_turn, 1)
                        nc.gpsimd.indirect_dma_start(out=sum_tab[:, :], out_offset=bass.IndirectOffsetOnAxis(ap=d_once[:, 0:1], axis=0),
                                                     in_=new[:, :], in_offset=None, bounds_check=N - 1,
                                                     oob_is_err=False).then_inc(stored, 16)
                    pool.wait_ge(stored, NT * 16)

                @gblock.tensor
                def _(pe):
                    with pe.Fori(0, NT) as t:
                        pe.wait_ge(z_ready, t + 1)
                        pe.sem_inc(g_turn, 1)
                        nc.tensor.transpose(bank[0][0:H1, 0:P], z_e[:], ident[:]).then_inc(t1, 1)
                        pe.wait_ge(r1, t + 1)
                        nc.tensor.matmul(bank[1][:, 0:P], w2[:], g1[:], start=True, stop=True).then_inc(t2, 1)
                        pe.wait_ge(r2, t + 1)
                        nc.tensor.matmul(bank[2][:, 0:H3], ones_b[:], b_k[:, 0, :], start=True, stop=False)
                        nc.tensor.matmul(bank[2][:, 0:H3], g2[:], w3[:], start=False, stop=True).then_inc(t3, 1)
                        pe.wait_ge(r3, t + 1)
                        nc.tensor.matmul(bank[3][:, 0:HX], S[:], g3[:], start=True, stop=True).then_inc(t4, 1)
                    with pe.Fori(0, NC) as c:
                        pe.wait_ge(one_ready, c + 1)
                        nc.tensor.transpose(bank[4][0:HX, 0:NP], s_one[:], ident[0:NP, 0:NP]).then_inc(one_tr, 1)

                @gblock.scalar
                def _(act):
                    act.wait_ge(low_set, 3)
                    with act.Fori(0, NT) as t:
                        act.wait_ge(t1, t + 1)
                        nc.scalar.activation(g1[:], bank[0][0:H1, 0:P], ACT.Relu).then_inc(r1, 1)
                        act.wait_ge(t2, t + 1)
                        nc.scalar.activation(g2[:], bank[1][:, 0:P], ACT.Relu, bias=b2c[:]).then_inc(r2, 1)
                        act.wait_ge(t3, t + 1)
                        nc.scalar.activation(g3[:, 0:H3], bank[2][:, 0:H3], ACT.Relu).then_inc(r3, 1)

                @gblock.vector
                def _(dve):
                    LINKS = 7

                    def step(t):
                        links = [0]

                        def link(ins):
                            links[0] += 1
                            ins.then_inc(g_chain, 1)
                            dve.wait_ge(g_chain, t * LINKS + links[0])

                        dve.wait_ge(ids_in, t * 48 + 48)
                        nc.vector.tensor_scalar(d_clip[:], d_col[:], float(N - 1), None, ALU.min).then_inc(clip_ready, 1)
                        link(nc.vector.tensor_copy(d_f[:], d_col[:]))
                        link(nc.vector.tensor_scalar(S[:], d_row[:], d_f[:], None, ALU.is_equal))
                        dve.wait_ge(low_set, 3)
                        link(nc.vector.tensor_tensor(S_low[:], S[:], low[:], ALU.mult))
                        link(nc.vector.tensor_reduce(dup[:], S_low[:], AX.X, ALU.add))
                        link(nc.vector.scalar_tensor_tensor(out=d_once[:], in0=dup[:], scalar=float(PAD_DST), in1=d_col[:],
                                                            op0=ALU.mult, op1=ALU.add))
                        dve.wait_ge(rows_in, t * 48 + 48)
                        link(nc.vector.tensor_tensor(z_e[:], B_r[:], A_r[:, 2, :], ALU.add))
                        link(nc.vector.tensor_tensor(z_e[:], z_e[:], A_r[:, 1, :], ALU.add))
                        nc.vector.tensor_tensor(z_e[:], z_e[:], A_r[:, 0, :], ALU.add).then_inc(z_ready, 1)
                        assert links[0] == LINKS
                        dve.wait_ge(t4, t + 1)
                        nc.vector.tensor_tensor(new[:], bank[3][:, 0:HX], old[:], ALU.add).then_inc(new_ready, 1)

                    with dve.Fori(0, NT - 1) as t:
                        step(t)
                    dve.wait_ge(stored, (NT - 1) * 16)
                    nc.vector.memset(d_col[:], PAD_DST).then_inc(pad_ready, 1)
                    nc.vector.memset(d_row[:], PAD_DST).then_inc(pad_ready, 1)
                    step(NT - 1)
                    dve.wait_ge(all_in, 16)
                    dve.wait_ge(acc_zero, 16 * (N // ZC))
                    with dve.Fori(0, NC) as c:
                        nc.vector.tensor_copy(s_one[:], s_all[:, bass.ds(c, 1), :].rearrange("p c k -> p (c k)")).then_inc(one_ready, 1)
                        dve.wait_ge(one_tr, c + 1)
                        nc.vector.tensor_copy(acc.rearrange("k (p c) -> k c p", c=NC)[:, bass.ds(c, 1), :].rearrange("k c p -> k (c p)"),
                                              bank[4][0:HX, 0:NP]).then_inc(one_done, 1)
                    dve.wait_ge(one_done, NC)

        fin = ExitStack()
        with fin:
            NB = 10
            DX = DO + 1
            part = fin.enter_context(nc.sbuf_tensor("part", [HX, 2, NB, NP], fp32))
            cnt = fin.enter_context(nc.sbuf_tensor("cnt", [NP, 2, NB], fp32))
            o_sb = fin.enter_context(nc.sbuf_tensor("o_sb", [NP, 2, NB * DO], fp32))
            part_ready, y_ready, y_read, o_ready2, n_chain = [
                fin.enter_context(nc.semaphore(n)) for n in ("part_ready", "y_ready", "y_read", "out_ready", "n_chain")]
            o_out = [fin.enter_context(nc.semaphore(f"o_out{i}")) for i in range(2)]
            out_v = out.rearrange("(p c) d -> p (c d)", p=NP)
            nblock = fin.enter_context(nc.Block())
            BATCHES = NC // NB

            def batches(eng, step):
                for n in range(2):
                    step(n, n)
                with eng.Fori(1, BATCHES // 2) as i:
                    for b in range(2):
                        step(i * 2 + b, b)

            @nblock.scalar
            def _(act):
                def step(n, b):
                    unless_zero(act, y_ready, n - 1)
                    nc.scalar.activation(part[:, b, :, :], acc.rearrange("k (p c) -> k c p", c=NC)[:, bass.ds(n * NB, NB), :],
                                         ACT.Copy).then_inc(part_ready, 1)
                batches(act, step)

            @nblock.tensor
            def _(pe):
                def step(n, b):
                    pe.wait_ge(part_ready, n + 1)
                    unless_zero(pe, y_read, n - 1)
                    for c in range(NB):
                        last = nc.tensor.matmul(bank[b][0:NP, c * DX:(c + 1) * DX], part[:, b, c, :], w4[:], start=True, stop=True)
                    last.then_inc(y_ready, 1)
                batches(pe, step)

            @nblock.vector
            def _(dve):
                def step(n, b):
                    y = bank[b][0:NP, 0:NB * DX].rearrange("p (c d) -> p c d", d=DX)
                    o = o_sb[:, b, :].rearrange("p (c d) -> p c d", d=DO)
                    dve.wait_ge(y_ready, n + 1)
                    nc.vector.tensor_scalar(cnt[:, b, :], y[:, :, DO], 1.0, None, ALU.max).then_inc(n_chain, 1)
                    dve.wait_ge(n_chain, n * 2 + 1)
                    nc.vector.reciprocal(cnt[:, b, :], cnt[:, b, :]).then_inc(n_chain, 1)
                    dve.wait_ge(n_chain, n * 2 + 2)
                    unless_zero(dve, o_out[b], (n - b) * 8)
                    nc.vector.tensor_tensor(o, y[:, :, 0:DO], cnt[:, b, :].unsqueeze(2).to_broadcast([NP, NB, DO]),
                                            ALU.mult).then_inc(y_read, 1)
                    dve.wait_ge(y_read, n + 1)
                    nc.vector.tensor_tensor(o_sb[:, b, :], o_sb[:, b, :], x_sb[:, bass.ds(n * (NB * D), NB * D)],
                                            ALU.add).then_inc(o_ready2, 1)
                batches(dve, step)

            @nblock.sync
            def _(sp):
                def step(n, b):
                    sp.wait_ge(o_ready2, n + 1)
                    sp.dma_start(out_v[:, bass.ds(n * (NB * DO), NB * DO)], o_sb[:, b, :]).then_inc(o_out[b], 16)
                batches(sp, step)
                sp.wait_ge(o_out[0], 16 * (BATCHES // 2))
                sp.wait_ge(o_out[1], 16 * (BATCHES // 2))


_INS = ["x", "src", "dst", "L0_gnn_W1", "L0_gnn_b1", "L0_gnn_W2", "L0_gnn_b2", "L0_gnn_W3", "L0_gnn_b3", "L0_gnn_W4", "L0_gnn_b4"]


def kernel(**inputs):
    import numpy as _np
    import concourse.bacc as _bacc
    from concourse import mybir as _mybir
    from concourse.bass_utils import run_bass_kernel_spmd as _run

    nc = _bacc.Bacc("TRN2", target_bir_lowering=False, num_devices=1)
    arrays, args = {}, []
    for name in _INS:
        a = _np.ascontiguousarray(inputs[name])
        arrays[f"in_{name}"] = a
        args.append(nc.dram_tensor(f"in_{name}", a.shape, _mybir.dt.from_np(a.dtype), kind="ExternalInput").ap())
    shape = arrays["in_x"].shape
    args.append(nc.dram_tensor("out_dram", shape, _mybir.dt.float32, kind="ExternalOutput").ap())
    build(nc, *args)
    r = _run(nc, [arrays], core_ids=[0])
    return r.results[0]["out_dram"]
```

```python
import concourse.bass as bass
from concourse import mybir
from concourse.alu_op_type import AluOpType as ALU
from contextlib import ExitStack



def build(nc, x, src, dst, W1, b1, W2, b2, W3, b3, W4, b4, out):
    fp32, bf16, i32 = mybir.dt.float32, mybir.dt.bfloat16, mybir.dt.int32
    ACT = mybir.ActivationFunctionType
    AX = mybir.AxisListType

    P = 128
    N, D = x.shape
    E = src.shape[0]
    H1, H2 = W2.shape
    H3 = W3.shape[1]
    DO = W4.shape[1]
    EPS = 1e-5

    NP, NC = 125, N // 125
    NQ = 4
    PW = 2 * NQ
    PN = -(-NC // PW)
    PB = [0, 1, 3, 6, 9, 11, PN]
    KC = len(PB) - 1
    CB = [min(b * PW, NC) for b in PB]
    CM = max(CB[k + 1] - CB[k] for k in range(KC))

    T = 4
    GE = T * P
    GR = 8
    G = -(-E // GE)
    QP = -(-G // GR)
    GA = QP * GR
    RL = GR * GE
    LAST = E - (QP - 1) * RL
    U = 8
    GP = U - 1
    GL = (G - U) // U
    W = 32
    PAD_DST = 1 << 20
    KA = 3 * W

    NT = -(-E // P)
    HX = H3 + 1
    DX = DO + 1

    def dram(name, shape, dt):
        return nc.dram_tensor(name, shape, dt, kind="Internal").ap()

    A_tab = dram("A_tab", (N * 3, H1), bf16)
    B_tab = dram("B_tab", (N, H1), fp32)
    base_tab = dram("base_tab", (GA,), i32)
    sum_tab = dram("sum_tab", (N, HX), fp32)

    ctx = ExitStack()
    with ctx:
        def sb(name, shape, dt=fp32):
            return ctx.enter_context(nc.sbuf_tensor(name, shape, dt))

        def sem(name):
            return ctx.enter_context(nc.semaphore(name))

        bank = [ctx.enter_context(nc.psum_tensor(f"bank{i}", [P, 512], fp32)) for i in range(8)]

        x_sb = sb("x_sb", [NP, NC * D])
        big = sb("big", [P, N])
        cen = big[0:NP, 0:NC * D]
        src_raw = big[0:QP, NC * D:NC * D + RL]
        dst_raw = big[0:QP, NC * D + RL:NC * D + 2 * RL]
        acc = big[0:DX, :]
        src_T = sb("src_T", [P, GA, T], i32)
        rel_T = sb("rel_T", [P, GA, T])
        base_bc = sb("base_bc", [P, GA], i32)
        base_row = sb("base_row", [1, GA], i32)
        ident = sb("ident", [P, P])
        iota_w = sb("iota_w", [P, T, W, 3])
        zeros = sb("zeros", [HX, 500])
        w2 = sb("w2", [H1, H2])
        w3 = sb("w3", [H2, H3])
        w4 = sb("w4", [HX, DX])
        b2c = sb("b2c", [H2, 1])
        b_row = sb("b_row", [1, 2, H3])
        b_r = sb("b_r", [1, 2, H3])
        b_p = sb("b_p", [1, 3, 2, H3], bf16)
        A_p = sb("A_p", [NP, NC, 3, H1], bf16)
        b_k = sb("b_k", [3, 2, H3], bf16)
        ones_b = sb("ones_b", [3, P], bf16)
        eps_c = sb("eps_c", [P, 1])
        flag_i = sb("flag_i", [1, 1], i32)
        idx = sb("idx", [P, U, T], i32)
        B_g = sb("B_g", [P, U, T, H1])

        x_in = [sem(f"x_in{k}") for k in range(KC)]
        src_in, dst_in, w_in, w2_in = sem("src_in"), sem("dst_in"), sem("w_in"), sem("w2_in")
        w1a_in = sem("w1a_in")
        bias_in = sem("bias_in")
        pool_const, pads_set, iota_ready, iota_mid = sem("pool_const"), sem("pads_set"), sem("iota_ready"), sem("iota_mid")
        dch = sem("dch")
        eps_ready, mean_ready, cen_ready, sq_ready = sem("eps_ready"), sem("mean_ready"), sem("cen_ready"), sem("sq_ready")
        ssq_ready, sd_ready, h_ready = sem("ssq_ready"), sem("sd_ready"), sem("h_ready")
        bdB_ready, bdA_ready = sem("bdB_ready"), sem("bdA_ready")
        src_fp, dst_fp, idx_tr, src_cp, dst_cp = sem("src_fp"), sem("dst_fp"), sem("idx_tr"), sem("src_cp"), sem("dst_cp")
        hT_tr, hT_cp, tabB_mm, tabB_cp, tabA_mm = sem("hT_tr"), sem("hT_cp"), sem("tabB_mm"), sem("tabB_cp"), sem("tabA_mm")
        BS = 3
        B_out = [sem(f"B_out{i}") for i in range(BS)]
        A_hi, A_rest, A_mid, A_lo, A_out = sem("A_hi"), sem("A_rest"), sem("A_mid"), sem("A_lo"), sem("A_out")
        base_ready, base_out, base_in, baseb_in = sem("base_ready"), sem("base_out"), sem("base_in"), sem("baseb_in")
        bad_ready, bad_mm, flag_ready = sem("bad_ready"), sem("bad_mm"), sem("flag_ready")
        b_ready, bk_in = sem("b_ready"), sem("bk_in")
        acc_zero, zero_set = sem("acc_zero"), sem("zero_set")
        idx_ready, turn = sem("idx_ready"), sem("turn")
        b_in = [sem(f"b_in{u}") for u in range(U)]

        def ids(g, u):
            nc.scalar.activation(idx[:, u, :], src_T[:, bass.ds(g, 1), :].rearrange("p g j -> p (g j)"),
                                 ACT.Copy).then_inc(idx_ready, 1)

        def tiles(g):
            return min(T, NT - g * T) if isinstance(g, int) else T

        def gather(pool, g, u):
            pool.wait_ge(idx_ready, g + 1)
            pool.sem_inc(turn, 1)
            for j in range(tiles(g)):
                nc.gpsimd.indirect_dma_start(
                    out=B_g[:, u, j, :], out_offset=None, in_=B_tab[:, :],
                    in_offset=bass.IndirectOffsetOnAxis(ap=idx[:, u, j:j + 1], axis=0)).then_inc(b_in[u], 16)

        prep = ExitStack()
        with prep:
            def psb(name, shape, dt=fp32):
                return prep.enter_context(nc.sbuf_tensor(name, shape, dt))

            sq = psb("sq", [NP, NC * D])
            st = psb("st", [NP, 4, NC])
            hT = psb("hT", [P, NC // NQ, NP])
            B_sb = psb("B_sb", [NP, BS, CM, H1])
            RS = 5
            A_r = psb("A_r", [NP, RS, PW, H1])
            w1a = psb("w1a", [P, H1])
            w1b = psb("w1b", [P, H1])
            w1_bd = psb("w1_bd", [P, 2, NQ, H1])
            base_i = psb("base_i", [QP, GR], i32)
            far = psb("far", [P, 2])
            bad = psb("bad", [P, 1])
            ones_f = psb("ones_f", [P, 1])
            scrap = psb("scrap", [1, 1])
            src_i = src_raw.bitcast(i32)
            dst_i = dst_raw.bitcast(i32)
            RH = RL // 2
            R0 = 7
            ZC = 2500

            def cols(t, k):
                return t[:, CB[k] * D:CB[k + 1] * D].rearrange("p (c d) -> p c d", d=D)

            def spread(t, k):
                return t[:, CB[k]:CB[k + 1]].unsqueeze(2).to_broadcast([NP, CB[k + 1] - CB[k], D])

            def pair(n):
                return slice(n * PW, min(n * PW + PW, NC))

            def quads(n):
                return range(2 * n, min(2 * n + 2, NC // NQ))

            def chunk_of(n):
                return max(k for k in range(KC) if PB[k] <= n)

            block = prep.enter_context(nc.Block(no_gpsimd_drain=True))
            hT_ps, B_ps = bank[2:4], bank[6:8]
            A_ps = bank[4:6] + bank[2:4]

            @block.gpsimd
            def _(pool):
                pad0 = (QP - 1) // 32 * 32
                nc.gpsimd.memset(src_i[pad0:QP, LAST:RL], 0).then_inc(pads_set, 1)
                nc.gpsimd.memset(dst_i[pad0:QP, LAST:RL], PAD_DST).then_inc(pads_set, 1)
                pool.wait_ge(pads_set, 2)
                nc.gpsimd.memset(ident[:], 0.0).then_inc(pool_const, 1)
                pool.wait_ge(pool_const, 1)
                nc.gpsimd.affine_select(out=ident[:], in_=ident[:], compare_op=ALU.not_equal, fill=1.0, base=0,
                                        pattern=[[-1, P]], channel_multiplier=1).then_inc(pool_const, 1)
                nc.gpsimd.memset(ones_b[:], 1.0).then_inc(pool_const, 1)
                nc.gpsimd.memset(ones_f[:], 1.0).then_inc(pool_const, 1)
                for k in range(KC):
                    pool.wait_ge(mean_ready, k + 1)
                    nc.gpsimd.tensor_tensor(cols(cen, k), cols(x_sb, k), spread(st[:, 1, :], k), ALU.add).then_inc(cen_ready, 1)
                nc.gpsimd.iota(iota_w[:], pattern=[[0, T], [1, W], [0, 3]], base=0, channel_multiplier=0,
                               allow_small_or_imprecise_dtypes=True).then_inc(iota_ready, 1)
                nc.gpsimd.memset(zeros[:], 0.0).then_inc(zero_set, 1)
                for b in range(BS):
                    pool.wait_ge(B_out[b], 16 * len(range(b, KC, BS)))
                for g in range(GP):
                    gather(pool, g, g)

            @block.sync
            def _(sp):
                def load_x(k):
                    sp.dma_start(cols(x_sb, k).rearrange("p c d -> p (c d)"),
                                 x.rearrange("(p c) d -> p (c d)", p=NP)[:, CB[k] * D:CB[k + 1] * D]).then_inc(x_in[k], 16)

                def load_ids(raw, arr, s):
                    sp.dma_start(raw[0:QP - 1, :], arr[0:(QP - 1) * RL].rearrange("(q e) -> q e", e=RL)).then_inc(s, 16)
                    sp.dma_start(raw[QP - 1:QP, 0:LAST], arr[(QP - 1) * RL:E].rearrange("(q e) -> q e", q=1)).then_inc(s, 16)

                load_x(0)
                for c in range(NQ // 2):
                    sp.dma_start(w1b[c * D:(c + 1) * D, :], W1[D:2 * D, :]).then_inc(w_in, 16)
                for k in range(1, KC):
                    load_x(k)
                sp.wait_ge(pads_set, 2)
                load_ids(src_i, src, src_in)
                load_ids(dst_i, dst, dst_in)
                sp.dma_start(b_row[:, 0, :], b3.rearrange("(o d) -> o d", o=1)).then_inc(bias_in, 16)
                sp.dma_start(b_row[:, 1, :], b1.rearrange("(o d) -> o d", o=1)).then_inc(bias_in, 16)
                for c in range(NQ):
                    sp.dma_start(w1a[c * D:(c + 1) * D, :], W1[0:D, :]).then_inc(w1a_in, 16)
                sp.dma_start(w2[:], W2).then_inc(w2_in, 16)
                sp.dma_start(w3[:], W3).then_inc(w2_in, 16)
                sp.dma_start(w4[0:H3, 0:DO], W4).then_inc(w2_in, 16)
                sp.dma_start(w4[H3:HX, 0:DO], b4.rearrange("(o d) -> o d", o=1)).then_inc(w2_in, 16)
                sp.dma_start(b2c[:], b2.rearrange("(d o) -> d o", o=1)).then_inc(w2_in, 16)
                Bv = B_tab.rearrange("(p c) d -> p c d", p=NP)
                for k in range(KC):
                    sp.wait_ge(tabB_cp, PB[k + 1])
                    sp.dma_start(Bv[:, CB[k]:CB[k + 1], :], B_sb[:, k % BS, 0:CB[k + 1] - CB[k], :]).then_inc(B_out[k % BS], 16)
                    if k == 2:
                        sp.wait_ge(b_ready, 1)
                        for i in range(3):
                            sp.dma_start(b_k[i:i + 1, :, :], b_p[:, i, :, :]).then_inc(bk_in, 16)
                sp.wait_ge(base_ready, 1)
                sp.dma_start(base_tab.rearrange("(q r) -> q r", r=GR), base_i[:]).then_inc(base_out, 16)
                sp.wait_ge(base_out, 16)
                sp.dma_start(base_bc[:], base_tab.partition_broadcast(P)).then_inc(baseb_in, 16)
                sp.dma_start(base_row[:], base_tab.rearrange("(o g) -> o g", o=1)).then_inc(base_in, 16)
                sp.wait_ge(zero_set, 1)
                sp.wait_ge(hT_tr, PN)
                sp.wait_ge(idx_tr, GR)
                dst_from = (NC * D + RL) // ZC * ZC
                dst_to = -(-(NC * D + 2 * RL) // ZC) * ZC

                def zero(c0, c1):
                    for c in range(c0, c1, ZC):
                        sp.dma_start(acc[:, c:c + ZC].rearrange("p (a b) -> p a b", b=500),
                                     zeros[0:DX, :].unsqueeze(1).to_broadcast([DX, ZC // 500, 500])).then_inc(acc_zero, 16)

                zero(0, dst_from)
                zero(dst_to, N)
                Av = A_tab.rearrange("(p c k) d -> p c k d", p=NP, k=3)
                for k in range(KC):
                    sp.wait_ge(A_lo, PB[k + 1])
                    sp.dma_start(Av[:, CB[k]:CB[k + 1], :, :], A_p[:, CB[k]:CB[k + 1], :, :]).then_inc(A_out, 16)
                sp.wait_ge(idx_tr, 2 * GR)
                zero(dst_from, dst_to)
                sp.wait_ge(base_in, 16)
                sp.wait_ge(w2_in, 16 * 5)

            @block.scalar
            def _(act):
                for c in range(NQ // 2, NQ):
                    act.dma_start(w1b[c * D:(c + 1) * D, :], W1[D:2 * D, :]).then_inc(w_in, 16)
                act.wait_ge(eps_ready, 1)
                nc.scalar.activation(scrap[:], eps_c[0:1, :], ACT.Sqrt)

                def square(k):
                    act.wait_ge(cen_ready, k + 1)
                    nc.scalar.activation(cols(sq, k), cols(cen, k), ACT.Square).then_inc(sq_ready, 1)

                def deviation(k):
                    act.wait_ge(ssq_ready, k + 1)
                    nc.scalar.activation(st[:, 3, CB[k]:CB[k + 1]], st[:, 2, CB[k]:CB[k + 1]], ACT.Sqrt,
                                         bias=eps_c[0:NP, :], scale=1.0 / D).then_inc(sd_ready, 1)

                def table_B(n):
                    if n < PN:
                        act.wait_ge(hT_tr, n + 1)
                        q = quads(n)
                        nc.scalar.activation(hT[:, q[0]:q[-1] + 1, :].rearrange("p q n -> p (q n)"), hT_ps[n % 2][:, 0:len(q) * NP],
                                             ACT.Copy).then_inc(hT_cp, 1)
                    m = n - 1
                    if 0 <= m < PN:
                        k = chunk_of(m)
                        c0, c1 = pair(m).start - CB[k], pair(m).stop - CB[k]
                        act.wait_ge(tabB_mm, m + 1)
                        if m == PB[k] and k >= BS:
                            act.wait_ge(B_out[k % BS], 16 * (k // BS))
                        nc.scalar.activation(B_sb[:, k % BS, c0:c1, :],
                                             B_ps[m % 2][0:NP, 0:(c1 - c0) * H1].rearrange("p (c w) -> p c w", w=H1),
                                             ACT.Copy).then_inc(tabB_cp, 1)
                    r = n - R0
                    if 0 <= r < GR:
                        act.wait_ge(idx_tr, r + 1)
                        nc.scalar.activation(src_T[:, :, :].rearrange("p (q r) j -> p r j q", r=GR)[:, r, :, :],
                                             bank[r % 2][:, 0:T * QP].rearrange("p (j q) -> p j q", j=T), ACT.Copy).then_inc(src_cp, 1)

                square(0)
                square(1)
                for k in range(KC):
                    deviation(k)
                    if k + 2 < KC:
                        square(k + 2)
                    if k >= 1:
                        for n in range(PB[k - 1], PB[k]):
                            table_B(n)
                for n in range(PB[KC - 1], max(PN + 1, R0 + GR)):
                    table_B(n)
                act.wait_ge(src_cp, GR)
                nc.scalar.activation(idx[:], src_T[:, 0:U, :], ACT.Copy).then_inc(idx_ready, U)
                for n in range(PN + 2):
                    if n < PN:
                        c = pair(n)
                        act.wait_ge(tabA_mm, n + 1)
                        nc.scalar.activation(A_p[:, c, 0, :], A_ps[n % 4][0:NP, 0:(c.stop - c.start) * H1].rearrange("p (c w) -> p c w", w=H1),
                                             ACT.Copy).then_inc(A_hi, 1)
                    m = n - 2
                    if m >= 0:
                        c = pair(m)
                        act.wait_ge(A_rest, m + 1)
                        nc.scalar.activation(A_p[:, c, 1, :], A_r[:, m % RS, 0:c.stop - c.start, :], ACT.Copy).then_inc(A_mid, 1)

            @block.tensor
            def _(pe):
                def index_rows(n, raw):
                    r = n % GR
                    if 2 <= n < GR + 2:
                        pe.wait_ge(src_cp, n - 1)
                    elif n >= GR + 2:
                        pe.wait_ge(dst_cp, n - GR - 1)
                    for j in range(T):
                        last = nc.tensor.transpose(bank[n % 2][:, j * QP:(j + 1) * QP],
                                                   raw[:, r * GE + j * P:r * GE + (j + 1) * P], ident[0:QP, 0:QP])
                    last.then_inc(idx_tr, 1)

                pe.wait_ge(pool_const, 4)
                pe.wait_ge(bdB_ready, 1)
                for n in range(max(PN + 1, R0 + GR)):
                    if n < PN:
                        pe.wait_ge(h_ready, chunk_of(n) + 1)
                        if n >= 2:
                            pe.wait_ge(hT_cp, n - 1)
                        for i, q in enumerate(quads(n)):
                            last = nc.tensor.transpose(hT_ps[n % 2][:, i * NP:(i + 1) * NP], cen[:, q * NQ * D:(q + 1) * NQ * D],
                                                       ident[0:NP, 0:NP])
                        last.then_inc(hT_tr, 1)
                    m = n - 1
                    if 0 <= m < PN:
                        pe.wait_ge(hT_cp, m + 1)
                        if m >= 2:
                            pe.wait_ge(tabB_cp, m - 1)
                        for i, q in enumerate(quads(m)):
                            last = nc.tensor.matmul(B_ps[m % 2][0:NP, i * NQ * H1:(i + 1) * NQ * H1], hT[:, q, :],
                                                    w1_bd[:, 1, :, :].rearrange("p c w -> p (c w)"), start=True, stop=True)
                        last.then_inc(tabB_mm, 1)
                    r = n - R0
                    if 0 <= r < GR:
                        pe.wait_ge(src_fp, 1 + (r >= GR // 2))
                        index_rows(r, src_raw)
                pe.wait_ge(bk_in, 48)
                pe.wait_ge(bdA_ready, 1)
                for n in range(max(PN, GR + 5)):
                    if n < PN:
                        if n >= 4:
                            pe.wait_ge(A_rest, n - 3)
                        w = (pair(n).stop - pair(n).start) * H1
                        nc.tensor.matmul(A_ps[n % 4][0:NP, 0:w], ones_b[:, 0:NP], b_k[:, 1:2, :].to_broadcast([3, w // H1, H1]), start=True, stop=False)
                        for i, q in enumerate(quads(n)):
                            last = nc.tensor.matmul(A_ps[n % 4][0:NP, i * NQ * H1:(i + 1) * NQ * H1], hT[:, q, :],
                                                    w1_bd[:, 0, :, :].rearrange("p c w -> p (c w)"), start=False, stop=(q == quads(n)[-1]))
                        last.then_inc(tabA_mm, 1)
                    r = n - 5
                    if 0 <= r < GR:
                        pe.wait_ge(dst_fp, 1)
                        index_rows(GR + r, dst_raw)
                pe.wait_ge(bad_ready, 1)
                pe.wait_ge(tabB_cp, PN)
                nc.tensor.matmul(bank[7][0:1, 0:1], bad[:], ones_f[:], start=True, stop=True).then_inc(bad_mm, 1)

            @block.vector
            def _(dve):
                chain = [0]

                def link(ins):
                    chain[0] += 1
                    ins.then_inc(dch, 1)
                    dve.wait_ge(dch, chain[0])

                def mean(k):
                    c = slice(CB[k], CB[k + 1])
                    dve.wait_ge(x_in[k], 16)
                    link(nc.vector.tensor_reduce(st[:, 0, c], cols(x_sb, k), AX.X, ALU.add))
                    nc.vector.tensor_scalar(st[:, 1, c], st[:, 0, c], -1.0 / D, None, ALU.mult).then_inc(mean_ready, 1)

                def sum_squares(k):
                    c = slice(CB[k], CB[k + 1])
                    dve.wait_ge(sq_ready, k + 1)
                    nc.vector.tensor_reduce(st[:, 2, c], cols(sq, k), AX.X, ALU.add).then_inc(ssq_ready, 1)

                def normalise(k):
                    c = slice(CB[k], CB[k + 1])
                    dve.wait_ge(sd_ready, k + 1)
                    link(nc.vector.reciprocal(st[:, 3, c], st[:, 3, c]))
                    nc.vector.scalar_tensor_tensor(out=cols(cen, k), in0=cols(cen, k), scalar=0.0, in1=spread(st[:, 3, :], k),
                                                   op0=ALU.max, op1=ALU.mult).then_inc(h_ready, 1)

                nc.vector.memset(eps_c[:], EPS).then_inc(eps_ready, 1)
                nc.vector.memset(w4[0:H3, DO:DO + 1], 0.0)
                nc.vector.memset(w4[H3:HX, DO:DO + 1], 1.0)
                nc.vector.memset(far[:], 0.0)
                link(nc.vector.memset(w1_bd[:], 0.0))
                mean(0)
                mean(1)
                sum_squares(0)
                mean(2)
                dve.wait_ge(w_in, 16 * NQ)
                for c in range(NQ):
                    rows = slice(c * D, (c + 1) * D)
                    last = nc.vector.tensor_copy(w1_bd[rows, 1, c, :], w1b[rows, :])
                last.then_inc(bdB_ready, 1)
                for k in range(KC):
                    if k + 1 < KC:
                        sum_squares(k + 1)
                    if k in (2, 3):
                        half = slice((k - 2) * RH, (k - 1) * RH)
                        dve.wait_ge(src_in, 32)
                        nc.vector.tensor_copy(src_raw[:, half], src_i[:, half]).then_inc(src_fp, 1)
                    if k == 4:
                        dve.wait_ge(bias_in, 32)
                        link(nc.vector.tensor_copy(b_p[:, 0, :, :], b_row[:]))
                        link(nc.vector.tensor_tensor(b_r[:], b_row[:], b_p[:, 0, :, :], ALU.subtract))
                        link(nc.vector.tensor_copy(b_p[:, 1, :, :], b_r[:]))
                        nc.vector.tensor_tensor(b_p[:, 2, :, :], b_r[:], b_p[:, 1, :, :], ALU.subtract).then_inc(b_ready, 1)
                    normalise(k)
                    if k + 3 < KC:
                        mean(k + 3)
                dve.wait_ge(dst_in, 32)
                nc.vector.tensor_scalar(base_i[:], dst_i.rearrange("q (r e) -> q r e", e=GE)[:, :, 0], float(N - W), None,
                                        ALU.min).then_inc(base_ready, 1)
                dve.wait_ge(w1a_in, 16 * NQ)
                for c in range(NQ):
                    rows = slice(c * D, (c + 1) * D)
                    last = nc.vector.tensor_tensor(w1_bd[rows, 0, c, :], w1a[rows, :], w1b[rows, :], ALU.subtract)
                last.then_inc(bdA_ready, 1)
                dve.wait_ge(base_ready, 1)
                nc.vector.tensor_copy(dst_raw, dst_i).then_inc(dst_fp, 1)
                dve.wait_ge(iota_ready, 1)
                nc.vector.tensor_scalar(iota_w[:], iota_w[:], -(W - 1) / 2, None, ALU.add).then_inc(iota_mid, 1)
                for n in range(PN + 3):
                    if n < PN:
                        c = pair(n)
                        w = c.stop - c.start
                        dve.wait_ge(A_hi, n + 1)
                        if n >= RS:
                            dve.wait_ge(A_lo, n - RS + 1)
                        nc.vector.tensor_tensor(A_r[:, n % RS, 0:w, :], A_ps[n % 4][0:NP, 0:w * H1].rearrange("p (c w) -> p c w", w=H1),
                                                A_p[:, c, 0, :], ALU.subtract).then_inc(A_rest, 1)
                    m = n - 3
                    if m >= 0:
                        c = pair(m)
                        dve.wait_ge(A_mid, m + 1)
                        nc.vector.tensor_tensor(A_p[:, c, 2, :], A_r[:, m % RS, 0:c.stop - c.start, :], A_p[:, c, 1, :],
                                                ALU.subtract).then_inc(A_lo, 1)
                    r = n - 4
                    if 0 <= r < GR:
                        if r == 0:
                            dve.wait_ge(baseb_in, 16)
                        dve.wait_ge(idx_tr, GR + r + 1)
                        nc.vector.scalar_tensor_tensor(out=rel_T[:, :, :].rearrange("p (q r) j -> p r j q", r=GR)[:, r, :, :],
                                                       in0=bank[r % 2][:, 0:T * QP].rearrange("p (j q) -> p j q", j=T),
                                                       scalar=-(W - 1) / 2,
                                                       in1=base_bc[:].rearrange("p (q r) -> p r q", r=GR)[:, r, :].unsqueeze(1).to_broadcast([P, T, QP]),
                                                       op0=ALU.add, op1=ALU.subtract).then_inc(dst_cp, 1)
                rel = rel_T[:, :, :].rearrange("p g j -> p (g j)")
                full, part = E // P, E % P
                dve.wait_ge(dst_cp, GR)
                link(nc.vector.tensor_reduce(far[:, 0:1], rel[:, 0:full], AX.X, ALU.max, apply_absolute_value=True))
                if part:
                    link(nc.vector.tensor_reduce(far[0:part, 1:2], rel[0:part, full:full + 1], AX.X, ALU.max,
                                                 apply_absolute_value=True))
                link(nc.vector.tensor_scalar(far[:], far[:], W / 2, None, ALU.is_ge))
                nc.vector.tensor_tensor(bad[:], far[:, 0:1], far[:, 1:2], ALU.max).then_inc(bad_ready, 1)
                dve.wait_ge(bad_mm, 1)
                nc.vector.tensor_copy(flag_i[:], bank[7][0:1, 0:1]).then_inc(flag_ready, 1)
                dve.wait_ge(iota_mid, 1)
                dve.wait_ge(flag_ready, 1)

        flag = nc.values_load(flag_i[0:1, 0:1], min_val=0, max_val=P)

        def unless_zero(eng, s, count):
            if not isinstance(count, int) or count > 0:
                eng.wait_ge(s, count)

        with nc.If(flag == 0):
            fast = ExitStack()
            with fast:
                def fsb(name, shape, dt=fp32):
                    return fast.enter_context(nc.sbuf_tensor(name, shape, dt))

                def fsem(name):
                    return fast.enter_context(nc.semaphore(name))

                A_w = fsb("A_w", [KA, U, H1], bf16)
                O = fsb("O", [P, U, T, W, 3])
                OT = fsb("OT", [KA, 2, GE], bf16)
                h1 = fsb("h1", [H1, 2, GE])
                h2 = fsb("h2", [H2, 2, GE])
                h3 = fsb("h3", [P, 2, T, HX])
                seg_sb = fsb("seg_sb", [HX, W])
                z1, z2, z3 = bank[0:2], bank[2:4], bank[4:6]
                ot_ps = bank[6]
                seg = [z3[b][0:HX, T * H3:T * H3 + W] for b in range(2)]
                y = bank[7][0:DX, 0:W]

                a_in = [fsem(f"a_in{u}") for u in range(U)]
                ones_set = fsem("ones_set")
                o_ready, ot_ready, otc_ready = fsem("o_ready"), fsem("ot_ready"), fsem("otc_ready")
                z1_ready, z2_ready, z3_ready, seg_ready = fsem("z1_ready"), fsem("z2_ready"), fsem("z3_ready"), fsem("seg_ready")
                segc_ready, y_ready = fsem("segc_ready"), fsem("y_mm")
                h1_ready, h2_ready, h3_ready, acc_done = fsem("h1_ready"), fsem("h2_ready"), fsem("h3_ready"), fsem("acc_done")

                def live(g):
                    return not isinstance(g, int) or 0 <= g < G

                def groups(eng, step, first=0, after=0):
                    for g in range(first, U):
                        step(g, g % U)
                    with eng.Fori(1, GL) as i:
                        for u in range(U):
                            step(i * U + u, u)
                    for g in range(GL * U, G + after):
                        step(g, g % U)

                fblock = fast.enter_context(nc.Block())

                @fblock.sync
                def _(sp):
                    def step(g, u):
                        unless_zero(sp, z1_ready, g - U + 1)
                        first = sp.value_load(base_row[0:1, bass.ds(g, 1)], min_val=0, max_val=N - W)
                        sp.dma_start(A_w[:, u, :], A_tab[bass.ds(first * 3, KA), :]).then_inc(a_in[u], 16)
                    sp.wait_ge(A_out, 16 * KC)
                    groups(sp, step)

                @fblock.gpsimd
                def _(pool):
                    groups(pool, lambda g, u: gather(pool, g, u), first=GP)

                @fblock.tensor
                def _(pe):
                    def step(g, u):
                        if live(g - 4):
                            pe.wait_ge(segc_ready, g - 3)
                            unless_zero(pe, acc_done, g - 4)
                            nc.tensor.matmul(y, w4[:], seg_sb[:], start=True, stop=True).then_inc(y_ready, 1)
                        if live(g - 2):
                            b = (u - 2) % 2
                            pe.wait_ge(h2_ready, g - 1)
                            unless_zero(pe, h3_ready, g - 3)
                            nc.tensor.matmul(z3[b][:, 0:T * H3], ones_b[:], b_k[:, 0:1, :].to_broadcast([3, T, H3]), start=True, stop=False)
                            for j in range(T):
                                last = nc.tensor.matmul(z3[b][:, j * H3:(j + 1) * H3], h2[:, b, j * P:(j + 1) * P], w3[:],
                                                        start=False, stop=(j == T - 1))
                            last.then_inc(z3_ready, 1)
                        if live(g - 3):
                            s, b = (u - 3) % U, (u - 3) % 2
                            pe.wait_ge(h3_ready, g - 2)
                            for j in range(T):
                                last = nc.tensor.matmul(seg[b], h3[:, b, j, :], O[:, s, j, :, 0],
                                                        start=(j == 0), stop=(j == T - 1))
                            last.then_inc(seg_ready, 1)
                        if live(g - 1):
                            b = (u - 1) % 2
                            pe.wait_ge(h1_ready, g)
                            unless_zero(pe, h2_ready, g - 2)
                            nc.tensor.matmul(z2[b][:, :], w2[:], h1[:, b, :], start=True, stop=True).then_inc(z2_ready, 1)
                        if live(g):
                            b = u % 2
                            pe.wait_ge(otc_ready, g + 1)
                            pe.wait_ge(a_in[u], (g - u) * (16 // U) + 16)
                            unless_zero(pe, h1_ready, g - 1)
                            nc.tensor.matmul(z1[b][0:H1, :], A_w[:, u, :], OT[:, b, :], start=True, stop=False)
                            pe.wait_ge(b_in[u], (g - u) * (16 * T // U) + 16 * tiles(g))
                            for j in range(T):
                                last = nc.tensor.matmul(z1[b][0:H1, j * P:(j + 1) * P], B_g[:, u, j, :], ident[:],
                                                        start=False, stop=(j == T - 1))
                            last.then_inc(z1_ready, 1)
                        if live(g + 1):
                            s = (u + 1) % U
                            pe.wait_ge(o_ready, g + 2)
                            unless_zero(pe, otc_ready, g + 1)
                            for j in range(T):
                                last = nc.tensor.transpose(ot_ps[0:KA, j * P:(j + 1) * P],
                                                           O[:, s, j, :, :].rearrange("p w k -> p (w k)"), ident[:])
                            last.then_inc(ot_ready, 1)
                    groups(pe, step, first=-1, after=4)

                @fblock.scalar
                def _(act):
                    def step(g, u):
                        if live(g - 2):
                            b = (u - 2) % 2
                            act.wait_ge(z3_ready, g - 1)
                            if isinstance(g, int) and g == 2:
                                act.wait_ge(ones_set, 1)
                            unless_zero(act, seg_ready, g - 3)
                            nc.scalar.activation(h3[:, b, :, 0:H3], z3[b][:, 0:T * H3].rearrange("p (j d) -> p j d", j=T),
                                                 ACT.Relu).then_inc(h3_ready, 1)
                        if live(g - 3):
                            act.wait_ge(seg_ready, g - 2)
                            unless_zero(act, y_ready, g - 3)
                            nc.scalar.activation(seg_sb[:], seg[(u - 3) % 2], ACT.Copy).then_inc(segc_ready, 1)
                        if live(g - 1):
                            b = (u - 1) % 2
                            act.wait_ge(z2_ready, g)
                            unless_zero(act, z3_ready, g - 2)
                            nc.scalar.activation(h2[:, b, :], z2[b][:, :], ACT.Relu, bias=b2c[:]).then_inc(h2_ready, 1)
                        if live(g):
                            b = u % 2
                            act.wait_ge(z1_ready, g + 1)
                            unless_zero(act, z2_ready, g - 1)
                            nc.scalar.activation(h1[:, b, :], z1[b][0:H1, :], ACT.Relu).then_inc(h1_ready, 1)
                            if live(g + U):
                                ids(g + U, u)
                    groups(act, step, after=3)

                @fblock.vector
                def _(dve):
                    nc.vector.memset(h3[:], 1.0).then_inc(ones_set, 1)

                    def step(g, u):
                        if live(g - 4):
                            if isinstance(g, int) and g == 4:
                                dve.wait_ge(acc_zero, 16 * (N // ZC))
                            dve.wait_ge(y_ready, g - 3)
                            unless_zero(dve, acc_done, g - 4)
                            first = dve.value_load(base_row[0:1, bass.ds(g - 4, 1)], min_val=0, max_val=N - W)
                            nc.vector.tensor_tensor(acc[:, bass.ds(first, W)], y, acc[:, bass.ds(first, W)],
                                                    ALU.add).then_inc(acc_done, 1)
                        if live(g + 1):
                            s, b = (u + 1) % U, (u + 1) % 2
                            nc.vector.tensor_tensor(O[:, s, :, :, :].rearrange("p j w k -> p j (w k)"),
                                                    rel_T[:, bass.ds(g + 1, 1), :].rearrange("p g j -> p (g j)").unsqueeze(2).to_broadcast([P, T, KA]),
                                                    iota_w[:].rearrange("p j w k -> p j (w k)"), ALU.is_equal).then_inc(o_ready, 1)
                            dve.wait_ge(ot_ready, g + 2)
                            unless_zero(dve, z1_ready, g)
                            nc.vector.tensor_copy(OT[:, b, :], ot_ps[0:KA, :]).then_inc(otc_ready, 1)
                    groups(dve, step, first=-1, after=4)
                    dve.wait_ge(acc_done, G)

        with nc.Else():
            gen = ExitStack()
            with gen:
                def gsb(name, shape, dt=fp32):
                    return gen.enter_context(nc.sbuf_tensor(name, shape, dt))

                def gsem(name):
                    return gen.enter_context(nc.semaphore(name))

                s_col = gsb("s_col", [P, 1], i32)
                d_col = gsb("d_col", [P, 1], i32)
                d_row = gsb("d_row", [P, P], i32)
                d_clip = gsb("d_clip", [P, 1], i32)
                d_f = gsb("d_f", [P, 1])
                S = gsb("S", [P, P])
                S_low = gsb("S_low", [P, P])
                low = gsb("low", [P, P])
                dup = gsb("dup", [P, 1])
                d_once = gsb("d_once", [P, 1], i32)
                B_r = gsb("B_r", [P, H1])
                A_r = gsb("A_r2", [P, 3, H1], bf16)
                z_e = gsb("z_e", [P, H1])
                g1 = gsb("g1", [H1, P])
                g2 = gsb("g2", [H2, P])
                g3 = gsb("g3", [P, HX])
                old = gsb("old", [P, HX])
                new = gsb("new", [P, HX])
                s_all = gsb("s_all", [NP, NC, HX])
                s_one = gsb("s_one", [NP, HX])
                s_oneT = gsb("s_oneT", [HX, NP])

                one_T, one_y = gsem("one_T"), gsem("one_y")
                g_turn, pad_ready = gsem("g_turn"), gsem("pad_ready")
                low_set, tab_zero, ids_in, clip_ready, rows_in, g_chain = (
                    gsem("low_set"), gsem("tab_zero"), gsem("ids_in"), gsem("clip_ready"), gsem("rows_in"), gsem("g_chain"))
                z_ready, t1, r1, t2, r2, t3, r3, t4 = [gsem(n) for n in ("z_ready", "t1", "r1", "t2", "r2", "t3", "r3", "t4")]
                new_ready, stored, all_in, one_ready, one_tr, one_done = [
                    gsem(n) for n in ("new_ready", "stored", "all_in", "one_ready", "one_tr", "one_done")]
                A_rows = A_tab.rearrange("(n k) d -> n (k d)", k=3)

                gblock = gen.enter_context(nc.Block())

                @gblock.sync
                def _(sp):
                    sp.dma_start(sum_tab.rearrange("n k -> (n k)").rearrange("(p a b) -> p a b", p=HX, b=500),
                                 zeros[:].unsqueeze(1).to_broadcast([HX, N // 500, 500])).then_inc(tab_zero, 16)

                    def step(t, n):
                        sp.wait_ge(stored, t * 16)
                        sp.dma_start(s_col[0:n, :], src[bass.ds(t * P, n)].rearrange("(p o) -> p o", o=1)).then_inc(ids_in, 16)
                        sp.dma_start(d_col[0:n, :], dst[bass.ds(t * P, n)].rearrange("(p o) -> p o", o=1)).then_inc(ids_in, 16)
                        sp.dma_start(d_row[:, 0:n], dst[bass.ds(t * P, n)].partition_broadcast(P)).then_inc(ids_in, 16)

                    with sp.Fori(0, NT - 1) as t:
                        step(t, P)
                    sp.wait_ge(pad_ready, 2)
                    step(NT - 1, E - (NT - 1) * P)
                    sp.wait_ge(stored, NT * 16)
                    sp.dma_start(s_all[:], sum_tab.rearrange("(p c) k -> p c k", p=NP)).then_inc(all_in, 16)

                @gblock.gpsimd
                def _(pool):
                    nc.gpsimd.memset(low[:], 1.0).then_inc(low_set, 1)
                    pool.wait_ge(low_set, 1)
                    nc.gpsimd.affine_select(out=low[:], in_=low[:], compare_op=ALU.is_gt, fill=0.0, base=0,
                                            pattern=[[-1, P]], channel_multiplier=1).then_inc(low_set, 1)
                    nc.gpsimd.memset(g3[:], 1.0).then_inc(low_set, 1)
                    pool.wait_ge(A_out, 16 * KC)
                    with pool.Fori(0, NT) as t:
                        pool.wait_ge(clip_ready, t + 1)
                        pool.wait_ge(tab_zero, 16)
                        pool.sem_inc(g_turn, 1)
                        for o, tab, i in ((B_r[:, :], B_tab[:, :], s_col), (A_r[:].rearrange("p k d -> p (k d)"), A_rows[:, :], d_clip),
                                          (old[:, :], sum_tab[:, :], d_clip)):
                            nc.gpsimd.indirect_dma_start(out=o, out_offset=None, in_=tab,
                                                         in_offset=bass.IndirectOffsetOnAxis(ap=i[:, 0:1], axis=0)).then_inc(rows_in, 16)
                        pool.wait_ge(new_ready, t + 1)
                        pool.sem_inc(g_turn, 1)
                        nc.gpsimd.indirect_dma_start(out=sum_tab[:, :], out_offset=bass.IndirectOffsetOnAxis(ap=d_once[:, 0:1], axis=0),
                                                     in_=new[:, :], in_offset=None, bounds_check=N - 1,
                                                     oob_is_err=False).then_inc(stored, 16)
                    pool.wait_ge(stored, NT * 16)

                @gblock.tensor
                def _(pe):
                    with pe.Fori(0, NT) as t:
                        pe.wait_ge(z_ready, t + 1)
                        pe.sem_inc(g_turn, 1)
                        nc.tensor.transpose(bank[0][0:H1, 0:P], z_e[:], ident[:]).then_inc(t1, 1)
                        pe.wait_ge(r1, t + 1)
                        nc.tensor.matmul(bank[1][:, 0:P], w2[:], g1[:], start=True, stop=True).then_inc(t2, 1)
                        pe.wait_ge(r2, t + 1)
                        nc.tensor.matmul(bank[2][:, 0:H3], ones_b[:], b_k[:, 0, :], start=True, stop=False)
                        nc.tensor.matmul(bank[2][:, 0:H3], g2[:], w3[:], start=False, stop=True).then_inc(t3, 1)
                        pe.wait_ge(r3, t + 1)
                        nc.tensor.matmul(bank[3][:, 0:HX], S[:], g3[:], start=True, stop=True).then_inc(t4, 1)
                    with pe.Fori(0, NC) as c:
                        pe.wait_ge(one_ready, c + 1)
                        nc.tensor.transpose(bank[4][0:HX, 0:NP], s_one[:], ident[0:NP, 0:NP]).then_inc(one_tr, 1)
                        pe.wait_ge(one_T, c + 1)
                        nc.tensor.matmul(bank[5][0:DX, 0:NP], w4[:], s_oneT[:], start=True, stop=True).then_inc(one_y, 1)

                @gblock.scalar
                def _(act):
                    act.wait_ge(low_set, 3)
                    with act.Fori(0, NT) as t:
                        act.wait_ge(t1, t + 1)
                        nc.scalar.activation(g1[:], bank[0][0:H1, 0:P], ACT.Relu).then_inc(r1, 1)
                        act.wait_ge(t2, t + 1)
                        nc.scalar.activation(g2[:], bank[1][:, 0:P], ACT.Relu, bias=b2c[:]).then_inc(r2, 1)
                        act.wait_ge(t3, t + 1)
                        nc.scalar.activation(g3[:, 0:H3], bank[2][:, 0:H3], ACT.Relu).then_inc(r3, 1)

                @gblock.vector
                def _(dve):
                    LINKS = 7

                    def step(t):
                        links = [0]

                        def link(ins):
                            links[0] += 1
                            ins.then_inc(g_chain, 1)
                            dve.wait_ge(g_chain, t * LINKS + links[0])

                        dve.wait_ge(ids_in, t * 48 + 48)
                        nc.vector.tensor_scalar(d_clip[:], d_col[:], float(N - 1), None, ALU.min).then_inc(clip_ready, 1)
                        link(nc.vector.tensor_copy(d_f[:], d_col[:]))
                        link(nc.vector.tensor_scalar(S[:], d_row[:], d_f[:], None, ALU.is_equal))
                        dve.wait_ge(low_set, 3)
                        link(nc.vector.tensor_tensor(S_low[:], S[:], low[:], ALU.mult))
                        link(nc.vector.tensor_reduce(dup[:], S_low[:], AX.X, ALU.add))
                        link(nc.vector.scalar_tensor_tensor(out=d_once[:], in0=dup[:], scalar=float(PAD_DST), in1=d_col[:],
                                                            op0=ALU.mult, op1=ALU.add))
                        dve.wait_ge(rows_in, t * 48 + 48)
                        link(nc.vector.tensor_tensor(z_e[:], B_r[:], A_r[:, 2, :], ALU.add))
                        link(nc.vector.tensor_tensor(z_e[:], z_e[:], A_r[:, 1, :], ALU.add))
                        nc.vector.tensor_tensor(z_e[:], z_e[:], A_r[:, 0, :], ALU.add).then_inc(z_ready, 1)
                        assert links[0] == LINKS
                        dve.wait_ge(t4, t + 1)
                        nc.vector.tensor_tensor(new[:], bank[3][:, 0:HX], old[:], ALU.add).then_inc(new_ready, 1)

                    with dve.Fori(0, NT - 1) as t:
                        step(t)
                    dve.wait_ge(stored, (NT - 1) * 16)
                    nc.vector.memset(d_col[:], PAD_DST).then_inc(pad_ready, 1)
                    nc.vector.memset(d_row[:], PAD_DST).then_inc(pad_ready, 1)
                    step(NT - 1)
                    dve.wait_ge(all_in, 16)
                    dve.wait_ge(acc_zero, 16 * (N // ZC))
                    with dve.Fori(0, NC) as c:
                        nc.vector.tensor_copy(s_one[:], s_all[:, bass.ds(c, 1), :].rearrange("p c k -> p (c k)")).then_inc(one_ready, 1)
                        dve.wait_ge(one_tr, c + 1)
                        nc.vector.tensor_copy(s_oneT[:], bank[4][0:HX, 0:NP]).then_inc(one_T, 1)
                        dve.wait_ge(one_y, c + 1)
                        nc.vector.tensor_copy(acc.rearrange("k (p c) -> k c p", c=NC)[:, bass.ds(c, 1), :].rearrange("k c p -> k (c p)"),
                                              bank[5][0:DX, 0:NP]).then_inc(one_done, 1)
                    dve.wait_ge(one_done, NC)

        fin = ExitStack()
        with fin:
            NB = 10
            part = fin.enter_context(nc.sbuf_tensor("part", [DX, 2, NB, NP], fp32))
            cnt = fin.enter_context(nc.sbuf_tensor("cnt", [NP, 2, NB], fp32))
            o_sb = fin.enter_context(nc.sbuf_tensor("o_sb", [NP, NC * DO], fp32))
            part_ready, y_ready, y_read, o_ready2, n_chain, n_turn = [
                fin.enter_context(nc.semaphore(n)) for n in ("part_ready", "y_ready", "y_read", "out_ready", "n_chain", "n_turn")]
            o_out = fin.enter_context(nc.semaphore("o_out"))
            out_v = out.rearrange("(p c) d -> p (c d)", p=NP)
            nblock = fin.enter_context(nc.Block())
            BATCHES = NC // NB

            def batches(eng, step):
                for n in range(2):
                    step(n, n)
                with eng.Fori(1, BATCHES // 2) as i:
                    for b in range(2):
                        step(i * 2 + b, b)

            @nblock.scalar
            def _(act):
                def step(n, b):
                    unless_zero(act, y_ready, n - 1)
                    nc.scalar.activation(part[:, b, :, :], acc.rearrange("k (p c) -> k c p", c=NC)[:, bass.ds(n * NB, NB), :],
                                         ACT.Copy).then_inc(part_ready, 1)
                batches(act, step)

            @nblock.tensor
            def _(pe):
                def step(n, b):
                    pe.wait_ge(part_ready, n + 1)
                    unless_zero(pe, y_read, n - 1)
                    pe.sem_inc(n_turn, 1)
                    for c in range(NB):
                        last = nc.tensor.transpose(bank[b][0:NP, c * DX:(c + 1) * DX], part[:, b, c, :], ident[0:DX, 0:DX])
                    last.then_inc(y_ready, 1)
                batches(pe, step)

            @nblock.vector
            def _(dve):
                def step(n, b):
                    y = bank[b][0:NP, 0:NB * DX].rearrange("p (c d) -> p c d", d=DX)
                    o = o_sb[:, bass.ds(n * (NB * DO), NB * DO)].rearrange("p (c d) -> p c d", d=DO)
                    dve.wait_ge(y_ready, n + 1)
                    nc.vector.tensor_scalar(cnt[:, b, :], y[:, :, DO], 1.0, None, ALU.max).then_inc(n_chain, 1)
                    dve.wait_ge(n_chain, n * 2 + 1)
                    nc.vector.reciprocal(cnt[:, b, :], cnt[:, b, :]).then_inc(n_chain, 1)
                    dve.wait_ge(n_chain, n * 2 + 2)
                    nc.vector.tensor_tensor(o, y[:, :, 0:DO], cnt[:, b, :].unsqueeze(2).to_broadcast([NP, NB, DO]),
                                            ALU.mult).then_inc(y_read, 1)
                batches(dve, step)

            @nblock.gpsimd
            def _(pool):
                def step(n, b):
                    pool.wait_ge(y_read, n + 1)
                    o = o_sb[:, bass.ds(n * (NB * DO), NB * DO)]
                    nc.gpsimd.tensor_tensor(o, o, x_sb[:, bass.ds(n * (NB * D), NB * D)],
                                            ALU.add).then_inc(o_ready2, 1)
                batches(pool, step)

            @nblock.sync
            def _(sp):
                def step(n, b):
                    sp.wait_ge(o_ready2, n + 1)
                    sp.dma_start(out_v[:, bass.ds(n * (NB * DO), NB * DO)], o_sb[:, bass.ds(n * (NB * DO), NB * DO)]).then_inc(o_out, 16)
                batches(sp, step)
                sp.wait_ge(o_out, 16 * BATCHES)


_INS = ["x", "src", "dst", "L0_gnn_W1", "L0_gnn_b1", "L0_gnn_W2", "L0_gnn_b2", "L0_gnn_W3", "L0_gnn_b3", "L0_gnn_W4", "L0_gnn_b4"]


def kernel(**inputs):
    import numpy as _np
    import concourse.bacc as _bacc
    from concourse import mybir as _mybir
    from concourse.bass_utils import run_bass_kernel_spmd as _run

    nc = _bacc.Bacc("TRN2", target_bir_lowering=False, num_devices=1)
    arrays, args = {}, []
    for name in _INS:
        a = _np.ascontiguousarray(inputs[name])
        arrays[f"in_{name}"] = a
        args.append(nc.dram_tensor(f"in_{name}", a.shape, _mybir.dt.from_np(a.dtype), kind="ExternalInput").ap())
    shape = arrays["in_x"].shape
    args.append(nc.dram_tensor("out_dram", shape, _mybir.dt.float32, kind="ExternalOutput").ap())
    build(nc, *args)
    r = _run(nc, [arrays], core_ids=[0])
    return r.results[0]["out_dram"]
```
